# Optimizing a Trainium2 kernel written in Bass

```python
import numpy as np
import jax
import jax.numpy as jnp

def _softmax(x, axis=-1):
    return jax.nn.softmax(x, axis=axis)

def _gelu(x):
    return jax.nn.gelu(x, approximate=True)

def _silu(x):
    return jax.nn.silu(x)

def _sigmoid(x):
    return jax.nn.sigmoid(x)

def _layernorm(x, axis=-1, eps=1e-05):
    m = jnp.mean(x, axis=axis, keepdims=True)
    v = jnp.var(x, axis=axis, keepdims=True)
    return (x - m) / jnp.sqrt(v + eps)

def _scatter_add(tgt, idx, src, axis=0):
    return tgt.at[idx].add(src)

def _segment_sum(src, seg, n):
    return jax.ops.segment_sum(src, seg, n)
kernel_name = 'mk_hybrid_d2_jaxref_r8_d1c876'

def setup_inputs(seed: int=0):
    np.random.seed(seed)
    _w = jnp.asarray

    def _L0_attn_a_setup():
        import jax, jax.numpy as jnp
        import numpy as np
        from jax import lax
        B_SZ, L, D_HID = (4, 512, 256)
        H, N, K, DT_RANK = (32, 16, 4, 128)
        D_INNER = H * N
        key = jax.random.key(seed)
        ks = jax.random.split(key, 12)
        s = 0.02
        inp = {'hidden_states': jax.random.normal(ks[0], (B_SZ, L, D_HID), jnp.float32), 'W_in_x': jax.random.normal(ks[1], (D_INNER, D_HID), jnp.float32) * s, 'W_in_z': jax.random.normal(ks[2], (D_INNER, D_HID), jnp.float32) * s, 'conv_w': jax.random.normal(ks[3], (D_INNER, 1, K), jnp.float32) * 0.1, 'conv_b': jax.random.normal(ks[4], (D_INNER,), jnp.float32) * 0.01, 'W_param': jax.random.normal(ks[5], (DT_RANK + 2 * H * N, D_INNER), jnp.float32) * s, 'W_dt': jax.random.normal(ks[6], (H, DT_RANK), jnp.float32) * s, 'b_dt': jnp.log(jax.random.uniform(ks[7], (H,), jnp.float32, 0.001, 0.01)), 'A_log': jnp.log(jax.random.uniform(ks[8], (H, N), jnp.float32, 0.1, 0.9)), 'D': jnp.ones((D_INNER,), jnp.float32), 'W_out': jax.random.normal(ks[9], (D_HID, D_INNER), jnp.float32) * s}
        return inp
    _L0_attn_a_in = _L0_attn_a_setup()

    def _L0_attn_b_setup():
        import jax, jax.numpy as jnp
        import numpy as np
        DIMS = 256
        HEAD = 16
        HD = DIMS // HEAD
        HD2 = HD // 2
        B, C = (1, 256)

        def layernorm(x, g, b, eps=1e-05):
            mu = x.mean(-1, keepdims=True)
            var = x.var(-1, keepdims=True)
            return (x - mu) / jnp.sqrt(var + eps) * g + b

        def rotary_freqs():
            f = (8000.0 / 200.0) ** jnp.linspace(0.0, 1.0, HD2) * 200.0 / 1000.0
            return 200.0 * f / 1000.0

        def apply_rotary(y, xa):
            t = jnp.arange(y.shape[2], dtype=jnp.float32)
            ang = jnp.einsum('i,j->ij', t, rotary_freqs())
            m = jnp.linalg.norm(xa, axis=-1)
            rr = (m[..., None] * jnp.cos(ang))[:, None]
            ri = (m[..., None] * jnp.sin(ang))[:, None]
            yp = y.reshape(*y.shape[:-1], HD2, 2)
            yr, yi = (yp[..., 0], yp[..., 1])
            out_r = yr * rr - yi * ri
            out_i = yr * ri + yi * rr
            return jnp.stack([out_r, out_i], axis=-1).reshape(y.shape)
        key = jax.random.key(seed)
        ks = jax.random.split(key, 4)
        s = 0.02
        return {'x': jax.random.normal(ks[0], (B, C, DIMS), jnp.float32), 'ln_q_g': jnp.ones((DIMS,), jnp.float32), 'ln_q_b': jnp.zeros((DIMS,), jnp.float32), 'Wq': jax.random.normal(ks[1], (DIMS, DIMS), jnp.float32) * s, 'bq': jnp.zeros((DIMS,), jnp.float32), 'ln_kv_g': jnp.ones((DIMS,), jnp.float32), 'ln_kv_b': jnp.zeros((DIMS,), jnp.float32), 'Wkv': jax.random.normal(ks[2], (DIMS, 2 * DIMS), jnp.float32) * s, 'bkv': jnp.zeros((2 * DIMS,), jnp.float32), 'ln_h_g': jnp.ones((HD,), jnp.float32), 'ln_h_b': jnp.zeros((HD,), jnp.float32), 'Wo': jax.random.normal(ks[3], (DIMS, DIMS), jnp.float32) * s, 'bo': jnp.zeros((DIMS,), jnp.float32)}
    _L0_attn_b_in = _L0_attn_b_setup()

    def _L0_ffn_setup():
        import jax, jax.numpy as jnp
        import numpy as np
        B, S, D = (2, 256, 256)
        E, TOP_K, H = (8, 2, 128)
        HS = 256
        key = jax.random.key(seed)
        ks = jax.random.split(key, 8)
        sc_d = 1.0 / np.sqrt(D)
        sc_h = 1.0 / np.sqrt(H)
        sc_hs = 1.0 / np.sqrt(HS)
        return {'hidden_states': jax.random.normal(ks[0], (B, S, D), jnp.float32), 'router_w': jax.random.normal(ks[1], (D, E), jnp.float32) * sc_d, 'w_gate': jax.random.normal(ks[2], (E, D, H), jnp.float32) * sc_d, 'w_up': jax.random.normal(ks[3], (E, D, H), jnp.float32) * sc_d, 'w_down': jax.random.normal(ks[4], (E, H, D), jnp.float32) * sc_h, 'sw_gate': jax.random.normal(ks[5], (D, HS), jnp.float32) * sc_d, 'sw_up': jax.random.normal(ks[6], (D, HS), jnp.float32) * sc_d, 'sw_down': jax.random.normal(ks[7], (HS, D), jnp.float32) * sc_hs}
    _L0_ffn_in = _L0_ffn_setup()

    def _L1_attn_a_setup():
        import jax, jax.numpy as jnp
        import numpy as np
        HID = 256
        H = 16
        D_NOPE = 128
        D_ROPE = 64
        D_Q = D_NOPE + D_ROPE
        D_V = 128
        QR = 192
        KVR = 64
        PH = 16
        PD = HID // PH
        THETA = 10000.0
        EPS = 1e-06

        def rmsnorm(x, w):
            var = jnp.mean(jnp.square(x), axis=-1, keepdims=True)
            return x * jax.lax.rsqrt(var + EPS) * w

        def rope_cos_sin(seq_len):
            inv_freq = 1.0 / THETA ** (jnp.arange(0, D_ROPE, 2, dtype=jnp.float32) / D_ROPE)
            t = jnp.arange(seq_len, dtype=jnp.float32)
            freqs = jnp.outer(t, inv_freq)
            emb = jnp.concatenate([freqs, freqs], -1)
            return (jnp.cos(emb), jnp.sin(emb))

        def rotate_half(x):
            x1, x2 = jnp.split(x, 2, axis=-1)
            return jnp.concatenate([-x2, x1], axis=-1)

        def apply_rope(x, cos, sin):
            return x * cos[None, None] + rotate_half(x) * sin[None, None]
        key = jax.random.key(seed)
        ks = jax.random.split(key, 12)

        def w(k, shape):
            return (jax.random.normal(k, shape, jnp.float32) / np.sqrt(shape[-1])).astype(jnp.float32)
        B, S = (2, 128)
        return {'hidden_states': jax.random.normal(ks[0], (B, S, HID), jnp.float32), 'q_a_w': w(ks[1], (QR, HID)), 'q_a_ln_w': jnp.ones((QR,), jnp.float32), 'q_b_w': w(ks[2], (H * D_Q, QR)), 'kv_a_w': w(ks[3], (KVR + H * D_ROPE, HID)), 'kv_a_ln_w': jnp.ones((KVR,), jnp.float32), 'kv_b_w': w(ks[4], (H * (D_NOPE + D_V), KVR)), 'o_w': w(ks[5], (HID, H * D_V)), 'sp_q_w': w(ks[6], (HID, HID)), 'sp_k_w': w(ks[7], (HID, HID)), 'sp_v_w': w(ks[8], (HID, HID)), 'sp_o_w': w(ks[9], (HID, HID)), 'gate_w': w(ks[10], (2, HID)), 'gate_b': jnp.zeros((2,), jnp.float32)}
    _L1_attn_a_in = _L1_attn_a_setup()

    def _L1_attn_b_setup():
        import jax, jax.numpy as jnp
        import numpy as np
        D_MODEL = 256
        N_QUERY = 4
        N_HEAD = 8
        D_HEAD = D_MODEL // (N_QUERY * N_HEAD)
        D_KV = D_HEAD * N_HEAD
        BATCH, SEQ = (2, 256)
        key = jax.random.key(seed)
        ks = jax.random.split(key, 5)
        w_scale = 1.0 / np.sqrt(D_MODEL).astype(np.float32)
        x = jax.random.normal(ks[0], (BATCH, SEQ, D_MODEL), jnp.float32)
        Wq = jax.random.normal(ks[1], (D_MODEL, D_MODEL), jnp.float32) * w_scale
        Wk = jax.random.normal(ks[2], (D_KV, D_MODEL), jnp.float32) * w_scale
        Wv = jax.random.normal(ks[3], (D_KV, D_MODEL), jnp.float32) * w_scale
        memory = jax.random.normal(ks[4], (D_KV, D_KV), jnp.float32) * 0.02
        memory_norm = jnp.ones((D_KV, 1), jnp.float32)
        memory_weight = jnp.ones((1,), jnp.float32)
        return dict(x=x, Wq=Wq, Wk=Wk, Wv=Wv, memory=memory, memory_norm=memory_norm, memory_weight=memory_weight)
    _L1_attn_b_in = _L1_attn_b_setup()

    def _L1_ffn_setup():
        import jax, jax.numpy as jnp
        import numpy as np
        B, S, H = (4, 128, 256)
        E, K, I, SI = (16, 4, 176, 704)

        def _silu_mul(gu, inter):
            return jax.nn.silu(gu[:, :inter]) * gu[:, inter:]
        key = jax.random.key(seed)
        ks = jax.random.split(key, 7)
        s = 0.02
        return {'hidden_states': jax.random.normal(ks[0], (B, S, H), jnp.float32), 'gate_w': jax.random.normal(ks[1], (E, H), jnp.float32) * s, 'expert_gate_up': jax.random.normal(ks[2], (E, 2 * I, H), jnp.float32) * s, 'expert_down': jax.random.normal(ks[3], (E, H, I), jnp.float32) * s, 'shared_gate_up': jax.random.normal(ks[4], (2 * SI, H), jnp.float32) * s, 'shared_down': jax.random.normal(ks[5], (H, SI), jnp.float32) * s, 'shared_gate_vec': jax.random.normal(ks[6], (1, H), jnp.float32) * s}
    _L1_ffn_in = _L1_ffn_setup()
    _d = {'L0_attn_a_hidden_states': _L0_attn_a_in['hidden_states'], 'L0_attn_a_W_in_x': _L0_attn_a_in['W_in_x'], 'L0_attn_a_W_in_z': _L0_attn_a_in['W_in_z'], 'L0_attn_a_conv_w': _L0_attn_a_in['conv_w'], 'L0_attn_a_conv_b': _L0_attn_a_in['conv_b'], 'L0_attn_a_W_param': _L0_attn_a_in['W_param'], 'L0_attn_a_W_dt': _L0_attn_a_in['W_dt'], 'L0_attn_a_b_dt': _L0_attn_a_in['b_dt'], 'L0_attn_a_A_log': _L0_attn_a_in['A_log'], 'L0_attn_a_D': _L0_attn_a_in['D'], 'L0_attn_a_W_out': _L0_attn_a_in['W_out'], 'L0_attn_b_ln_q_g': _L0_attn_b_in['ln_q_g'], 'L0_attn_b_ln_q_b': _L0_attn_b_in['ln_q_b'], 'L0_attn_b_Wq': _L0_attn_b_in['Wq'], 'L0_attn_b_bq': _L0_attn_b_in['bq'], 'L0_attn_b_ln_kv_g': _L0_attn_b_in['ln_kv_g'], 'L0_attn_b_ln_kv_b': _L0_attn_b_in['ln_kv_b'], 'L0_attn_b_Wkv': _L0_attn_b_in['Wkv'], 'L0_attn_b_bkv': _L0_attn_b_in['bkv'], 'L0_attn_b_ln_h_g': _L0_attn_b_in['ln_h_g'], 'L0_attn_b_ln_h_b': _L0_attn_b_in['ln_h_b'], 'L0_attn_b_Wo': _L0_attn_b_in['Wo'], 'L0_attn_b_bo': _L0_attn_b_in['bo'], 'L0_ffn_router_w': _L0_ffn_in['router_w'], 'L0_ffn_w_gate': _L0_ffn_in['w_gate'], 'L0_ffn_w_up': _L0_ffn_in['w_up'], 'L0_ffn_w_down': _L0_ffn_in['w_down'], 'L0_ffn_sw_gate': _L0_ffn_in['sw_gate'], 'L0_ffn_sw_up': _L0_ffn_in['sw_up'], 'L0_ffn_sw_down': _L0_ffn_in['sw_down'], 'L1_attn_a_q_a_w': _L1_attn_a_in['q_a_w'], 'L1_attn_a_q_a_ln_w': _L1_attn_a_in['q_a_ln_w'], 'L1_attn_a_q_b_w': _L1_attn_a_in['q_b_w'], 'L1_attn_a_kv_a_w': _L1_attn_a_in['kv_a_w'], 'L1_attn_a_kv_a_ln_w': _L1_attn_a_in['kv_a_ln_w'], 'L1_attn_a_kv_b_w': _L1_attn_a_in['kv_b_w'], 'L1_attn_a_o_w': _L1_attn_a_in['o_w'], 'L1_attn_a_sp_q_w': _L1_attn_a_in['sp_q_w'], 'L1_attn_a_sp_k_w': _L1_attn_a_in['sp_k_w'], 'L1_attn_a_sp_v_w': _L1_attn_a_in['sp_v_w'], 'L1_attn_a_sp_o_w': _L1_attn_a_in['sp_o_w'], 'L1_attn_a_gate_w': _L1_attn_a_in['gate_w'], 'L1_attn_a_gate_b': _L1_attn_a_in['gate_b'], 'L1_attn_b_Wq': _L1_attn_b_in['Wq'], 'L1_attn_b_Wk': _L1_attn_b_in['Wk'], 'L1_attn_b_Wv': _L1_attn_b_in['Wv'], 'L1_attn_b_memory': _L1_attn_b_in['memory'], 'L1_attn_b_memory_norm': _L1_attn_b_in['memory_norm'], 'L1_attn_b_memory_weight': _L1_attn_b_in['memory_weight'], 'L1_ffn_gate_w': _L1_ffn_in['gate_w'], 'L1_ffn_expert_gate_up': _L1_ffn_in['expert_gate_up'], 'L1_ffn_expert_down': _L1_ffn_in['expert_down'], 'L1_ffn_shared_gate_up': _L1_ffn_in['shared_gate_up'], 'L1_ffn_shared_down': _L1_ffn_in['shared_down'], 'L1_ffn_shared_gate_vec': _L1_ffn_in['shared_gate_vec']}
    _x0 = _d['L0_attn_a_hidden_states']
    _d['L0_attn_a_hidden_states'] = jax.random.normal(jax.random.fold_in(jax.random.key(seed), 1), (4, 512, 256), dtype=_x0.dtype)
    del _x0
    return _d

def reference(L0_attn_a_hidden_states, L0_attn_a_W_in_x, L0_attn_a_W_in_z, L0_attn_a_conv_w, L0_attn_a_conv_b, L0_attn_a_W_param, L0_attn_a_W_dt, L0_attn_a_b_dt, L0_attn_a_A_log, L0_attn_a_D, L0_attn_a_W_out, L0_attn_b_ln_q_g, L0_attn_b_ln_q_b, L0_attn_b_Wq, L0_attn_b_bq, L0_attn_b_ln_kv_g, L0_attn_b_ln_kv_b, L0_attn_b_Wkv, L0_attn_b_bkv, L0_attn_b_ln_h_g, L0_attn_b_ln_h_b, L0_attn_b_Wo, L0_attn_b_bo, L0_ffn_router_w, L0_ffn_w_gate, L0_ffn_w_up, L0_ffn_w_down, L0_ffn_sw_gate, L0_ffn_sw_up, L0_ffn_sw_down, L1_attn_a_q_a_w, L1_attn_a_q_a_ln_w, L1_attn_a_q_b_w, L1_attn_a_kv_a_w, L1_attn_a_kv_a_ln_w, L1_attn_a_kv_b_w, L1_attn_a_o_w, L1_attn_a_sp_q_w, L1_attn_a_sp_k_w, L1_attn_a_sp_v_w, L1_attn_a_sp_o_w, L1_attn_a_gate_w, L1_attn_a_gate_b, L1_attn_b_Wq, L1_attn_b_Wk, L1_attn_b_Wv, L1_attn_b_memory, L1_attn_b_memory_norm, L1_attn_b_memory_weight, L1_ffn_gate_w, L1_ffn_expert_gate_up, L1_ffn_expert_down, L1_ffn_shared_gate_up, L1_ffn_shared_down, L1_ffn_shared_gate_vec):

    def _L0_attn_a_ref(hidden_states, W_in_x, W_in_z, conv_w, conv_b, W_param, W_dt, b_dt, A_log, D, W_out):
        import jax, jax.numpy as jnp
        import numpy as np
        from jax import lax
        B_SZ, L, D_HID = (4, 512, 256)
        H, N, K, DT_RANK = (32, 16, 4, 128)
        D_INNER = H * N
        B, Lq, _ = hidden_states.shape
        x = hidden_states @ W_in_x.T
        z = hidden_states @ W_in_z.T
        xc = jnp.pad(x.transpose(0, 2, 1), ((0, 0), (0, 0), (K - 1, 0)))
        xconv = lax.conv_general_dilated(xc, conv_w, window_strides=(1,), padding='VALID', dimension_numbers=('NCH', 'OIH', 'NCH'), feature_group_count=D_INNER) + conv_b[None, :, None]
        x_act = jax.nn.silu(xconv.transpose(0, 2, 1))
        params = x_act @ W_param.T
        dt_feats = params[..., :DT_RANK]
        B_raw = params[..., DT_RANK:DT_RANK + H * N].reshape(B, Lq, H, N)
        C_raw = params[..., DT_RANK + H * N:].reshape(B, Lq, H, N)
        delta = jax.nn.softplus(dt_feats @ W_dt.T + b_dt)
        A = -jnp.exp(A_log)
        A_bar = jnp.exp(delta[..., None] * A)
        u = x_act.reshape(B, Lq, H, N)
        Bu = delta[..., None] * B_raw * u

        def step(h, inp):
            a, b, c = inp
            h = a * h + b
            return (h, c * h)
        h0 = jnp.zeros((B, H, N), x.dtype)
        _, ys = lax.scan(step, h0, (A_bar.transpose(1, 0, 2, 3), Bu.transpose(1, 0, 2, 3), C_raw.transpose(1, 0, 2, 3)))
        y = ys.transpose(1, 0, 2, 3).reshape(B, Lq, D_INNER)
        y = y + D * x_act
        y = y * jax.nn.silu(z)
        return y @ W_out.T

    def _L0_attn_b_ref(x, ln_q_g, ln_q_b, Wq, bq, ln_kv_g, ln_kv_b, Wkv, bkv, ln_h_g, ln_h_b, Wo, bo):
        import jax, jax.numpy as jnp
        import numpy as np
        DIMS = 256
        HEAD = 16
        HD = DIMS // HEAD
        HD2 = HD // 2
        B, C = (1, 256)

        def layernorm(x, g, b, eps=1e-05):
            mu = x.mean(-1, keepdims=True)
            var = x.var(-1, keepdims=True)
            return (x - mu) / jnp.sqrt(var + eps) * g + b

        def rotary_freqs():
            f = (8000.0 / 200.0) ** jnp.linspace(0.0, 1.0, HD2) * 200.0 / 1000.0
            return 200.0 * f / 1000.0

        def apply_rotary(y, xa):
            t = jnp.arange(y.shape[2], dtype=jnp.float32)
            ang = jnp.einsum('i,j->ij', t, rotary_freqs())
            m = jnp.linalg.norm(xa, axis=-1)
            rr = (m[..., None] * jnp.cos(ang))[:, None]
            ri = (m[..., None] * jnp.sin(ang))[:, None]
            yp = y.reshape(*y.shape[:-1], HD2, 2)
            yr, yi = (yp[..., 0], yp[..., 1])
            out_r = yr * rr - yi * ri
            out_i = yr * ri + yi * rr
            return jnp.stack([out_r, out_i], axis=-1).reshape(y.shape)
        b, c, d = x.shape
        q = (layernorm(x, ln_q_g, ln_q_b) @ Wq + bq).reshape(b, c, HEAD, HD).transpose(0, 2, 1, 3)
        kv = (layernorm(x, ln_kv_g, ln_kv_b) @ Wkv + bkv).reshape(b, c, 2, HEAD, HD)
        k = kv[:, :, 0].transpose(0, 2, 1, 3)
        v = kv[:, :, 1].transpose(0, 2, 1, 3)
        scale = HD ** (-0.25)
        q = q * scale
        k = k * scale
        q = apply_rotary(q, x)
        k = apply_rotary(k, x)
        qn = layernorm(q, ln_h_g, ln_h_b)
        kn = layernorm(k, ln_h_g, ln_h_b)
        logits = jnp.einsum('bhqd,bhkd->bhqk', qn, kn) / jnp.sqrt(jnp.float32(HD))
        att = jax.nn.softmax(logits, axis=-1)
        a = jnp.einsum('bhqk,bhkd->bhqd', att, v)
        a = a.transpose(0, 2, 1, 3).reshape(b, c, d)
        return a @ Wo + bo

    def _L0_ffn_ref(hidden_states, router_w, w_gate, w_up, w_down, sw_gate, sw_up, sw_down):
        import jax, jax.numpy as jnp
        import numpy as np
        B, S, D = (2, 256, 256)
        E, TOP_K, H = (8, 2, 128)
        HS = 256
        b, s, d = hidden_states.shape
        x = hidden_states.reshape(-1, d)
        T = x.shape[0]
        logits = x @ router_w
        probs = jax.nn.softmax(logits, axis=-1)
        topk_w, topk_idx = jax.lax.top_k(probs, TOP_K)
        topk_w = topk_w / jnp.sum(topk_w, axis=-1, keepdims=True)
        g = jnp.einsum('td,edh->teh', x, w_gate)
        u = jnp.einsum('td,edh->teh', x, w_up)
        h = jax.nn.silu(g) * u
        y = jnp.einsum('teh,ehd->ted', h, w_down)
        combine = jnp.zeros((T, E), dtype=x.dtype)
        combine = combine.at[jnp.arange(T)[:, None], topk_idx].add(topk_w)
        routed = jnp.einsum('te,ted->td', combine, y)
        sh = jax.nn.silu(hidden_states @ sw_gate) * (hidden_states @ sw_up)
        shared = sh @ sw_down
        return routed.reshape(b, s, d) + shared

    def _L1_attn_a_ref(hidden_states, q_a_w, q_a_ln_w, q_b_w, kv_a_w, kv_a_ln_w, kv_b_w, o_w, sp_q_w, sp_k_w, sp_v_w, sp_o_w, gate_w, gate_b):
        import jax, jax.numpy as jnp
        import numpy as np
        HID = 256
        H = 16
        D_NOPE = 128
        D_ROPE = 64
        D_Q = D_NOPE + D_ROPE
        D_V = 128
        QR = 192
        KVR = 64
        PH = 16
        PD = HID // PH
        THETA = 10000.0
        EPS = 1e-06

        def rmsnorm(x, w):
            var = jnp.mean(jnp.square(x), axis=-1, keepdims=True)
            return x * jax.lax.rsqrt(var + EPS) * w

        def rope_cos_sin(seq_len):
            inv_freq = 1.0 / THETA ** (jnp.arange(0, D_ROPE, 2, dtype=jnp.float32) / D_ROPE)
            t = jnp.arange(seq_len, dtype=jnp.float32)
            freqs = jnp.outer(t, inv_freq)
            emb = jnp.concatenate([freqs, freqs], -1)
            return (jnp.cos(emb), jnp.sin(emb))

        def rotate_half(x):
            x1, x2 = jnp.split(x, 2, axis=-1)
            return jnp.concatenate([-x2, x1], axis=-1)

        def apply_rope(x, cos, sin):
            return x * cos[None, None] + rotate_half(x) * sin[None, None]
        b, s, _ = hidden_states.shape
        dt = hidden_states.dtype
        q_mid = rmsnorm(hidden_states @ q_a_w.T, q_a_ln_w)
        q = (q_mid @ q_b_w.T).reshape(b, s, H, D_Q).transpose(0, 2, 1, 3)
        q_nope, q_pe = (q[..., :D_NOPE], q[..., D_NOPE:])
        kv_a = hidden_states @ kv_a_w.T
        kv_lora, k_pe_flat = (kv_a[..., :KVR], kv_a[..., KVR:])
        k_pe = k_pe_flat.reshape(b, s, H, D_ROPE).transpose(0, 2, 1, 3)
        kv = rmsnorm(kv_lora, kv_a_ln_w) @ kv_b_w.T
        kv = kv.reshape(b, s, H, D_NOPE + D_V).transpose(0, 2, 1, 3)
        k_nope, v = (kv[..., :D_NOPE], kv[..., D_NOPE:])
        cos, sin = rope_cos_sin(s)
        q_pe = apply_rope(q_pe, cos, sin)
        k_pe = apply_rope(k_pe, cos, sin)
        qf = jnp.concatenate([q_nope, q_pe], -1)
        kf = jnp.concatenate([k_nope, k_pe], -1)
        scale = D_Q ** (-0.5)
        scores = jnp.einsum('bhqd,bhkd->bhqk', qf, kf) * scale
        probs = jax.nn.softmax(scores.astype(jnp.float32), axis=-1).astype(dt)
        ctx = jnp.einsum('bhqk,bhkd->bhqd', probs, v)
        main_out = ctx.transpose(0, 2, 1, 3).reshape(b, s, H * D_V) @ o_w.T

        def split_heads(x):
            return x.reshape(b, s, PH, PD).transpose(0, 2, 1, 3)
        pq = split_heads(hidden_states @ sp_q_w.T)
        pk = split_heads(hidden_states @ sp_k_w.T)
        pv = split_heads(hidden_states @ sp_v_w.T)
        p_scores = jnp.einsum('bhqd,bhkd->bhqk', pq, pk) * PD ** (-0.5)
        p_probs = jax.nn.softmax(p_scores.astype(jnp.float32), axis=-1).astype(dt)
        p_ctx = jnp.einsum('bhqk,bhkd->bhqd', p_probs, pv)
        pattern_out = p_ctx.transpose(0, 2, 1, 3).reshape(b, s, HID) @ sp_o_w.T
        gates = jax.nn.softmax(hidden_states @ gate_w.T + gate_b, axis=-1)
        return gates[..., 0:1] * main_out + gates[..., 1:2] * pattern_out

    def _L1_attn_b_ref(x, Wq, Wk, Wv, memory, memory_norm, memory_weight):
        import jax, jax.numpy as jnp
        import numpy as np
        D_MODEL = 256
        N_QUERY = 4
        N_HEAD = 8
        D_HEAD = D_MODEL // (N_QUERY * N_HEAD)
        D_KV = D_HEAD * N_HEAD
        BATCH, SEQ = (2, 256)
        b, s, d = x.shape
        q = x @ Wq.T
        k = x @ Wk.T
        v = x @ Wv.T
        qh = q.reshape(b, s, N_QUERY, N_HEAD, D_HEAD)
        kh = k.reshape(b, s, N_HEAD, D_HEAD)
        vh = v.reshape(b, s, N_HEAD, D_HEAD)
        scale = np.float32(1.0 / np.sqrt(np.float32(D_HEAD)))
        scores = jnp.einsum('bsqhd,bthd->bqhst', qh, kh) * scale
        probs = jax.nn.softmax(scores, axis=-1)
        a_dot = jnp.einsum('bqhst,bthd->bsqhd', probs, vh)
        a_dot = a_dot.reshape(b, s, N_QUERY * N_HEAD, D_HEAD)
        sigma_q = jax.nn.elu(q.reshape(b, s, N_QUERY, D_KV))
        a_mem = sigma_q @ memory / (sigma_q @ memory_norm)
        a_mem = a_mem.reshape(b, s, N_QUERY * N_HEAD, D_HEAD)
        w = jax.nn.sigmoid(memory_weight)
        out = a_dot * (1.0 - w) + a_mem * w
        return out.reshape(b, s, D_MODEL)

    def _L1_ffn_ref(hidden_states, gate_w, expert_gate_up, expert_down, shared_gate_up, shared_down, shared_gate_vec):
        import jax, jax.numpy as jnp
        import numpy as np
        B, S, H = (4, 128, 256)
        E, K, I, SI = (16, 4, 176, 704)

        def _silu_mul(gu, inter):
            return jax.nn.silu(gu[:, :inter]) * gu[:, inter:]
        orig_shape = hidden_states.shape
        x = hidden_states.reshape(-1, H)
        router_logits = x @ gate_w.T
        routing_probs = jax.nn.softmax(router_logits.astype(jnp.float32), axis=-1)
        topk_w, topk_idx = jax.lax.top_k(routing_probs, K)
        topk_w = topk_w / topk_w.sum(axis=-1, keepdims=True)
        topk_w = topk_w.astype(x.dtype)
        combine = (jax.nn.one_hot(topk_idx, E, dtype=x.dtype) * topk_w[..., None]).sum(1)
        shared = _silu_mul(x @ shared_gate_up.T, SI) @ shared_down.T
        shared = shared * jax.nn.sigmoid(x @ shared_gate_vec.T)

        def step(acc, ew):
            w_gu, w_d, cw = ew
            h = _silu_mul(x @ w_gu.T, I)
            return (acc + h @ w_d.T * cw[:, None], None)
        acc0 = jnp.zeros_like(x)
        sparse, _ = jax.lax.scan(step, acc0, (expert_gate_up, expert_down, combine.T))
        return (shared + sparse).reshape(orig_shape)
    x = L0_attn_a_hidden_states
    x = x + _L0_attn_a_ref(_layernorm(x, axis=-1), L0_attn_a_W_in_x, L0_attn_a_W_in_z, L0_attn_a_conv_w, L0_attn_a_conv_b, L0_attn_a_W_param, L0_attn_a_W_dt, L0_attn_a_b_dt, L0_attn_a_A_log, L0_attn_a_D, L0_attn_a_W_out)
    x = x + _L0_ffn_ref(_layernorm(x, axis=-1), L0_ffn_router_w, L0_ffn_w_gate, L0_ffn_w_up, L0_ffn_w_down, L0_ffn_sw_gate, L0_ffn_sw_up, L0_ffn_sw_down)
    x = x + _L0_attn_b_ref(_layernorm(x, axis=-1), L0_attn_b_ln_q_g, L0_attn_b_ln_q_b, L0_attn_b_Wq, L0_attn_b_bq, L0_attn_b_ln_kv_g, L0_attn_b_ln_kv_b, L0_attn_b_Wkv, L0_attn_b_bkv, L0_attn_b_ln_h_g, L0_attn_b_ln_h_b, L0_attn_b_Wo, L0_attn_b_bo)
    x = x + _L0_ffn_ref(_layernorm(x, axis=-1), L0_ffn_router_w, L0_ffn_w_gate, L0_ffn_w_up, L0_ffn_w_down, L0_ffn_sw_gate, L0_ffn_sw_up, L0_ffn_sw_down)
    x = x + _L1_attn_a_ref(_layernorm(x, axis=-1), L1_attn_a_q_a_w, L1_attn_a_q_a_ln_w, L1_attn_a_q_b_w, L1_attn_a_kv_a_w, L1_attn_a_kv_a_ln_w, L1_attn_a_kv_b_w, L1_attn_a_o_w, L1_attn_a_sp_q_w, L1_attn_a_sp_k_w, L1_attn_a_sp_v_w, L1_attn_a_sp_o_w, L1_attn_a_gate_w, L1_attn_a_gate_b)
    x = x + _L1_ffn_ref(_layernorm(x, axis=-1), L1_ffn_gate_w, L1_ffn_expert_gate_up, L1_ffn_expert_down, L1_ffn_shared_gate_up, L1_ffn_shared_down, L1_ffn_shared_gate_vec)
    x = x + _L1_attn_b_ref(_layernorm(x, axis=-1), L1_attn_b_Wq, L1_attn_b_Wk, L1_attn_b_Wv, L1_attn_b_memory, L1_attn_b_memory_norm, L1_attn_b_memory_weight)
    x = x + _L1_ffn_ref(_layernorm(x, axis=-1), L1_ffn_gate_w, L1_ffn_expert_gate_up, L1_ffn_expert_down, L1_ffn_shared_gate_up, L1_ffn_shared_down, L1_ffn_shared_gate_vec)
    return x

_drawn_inputs = setup_inputs


def setup_inputs(seed=0):
    import zlib

    import numpy as np

    out = dict(_drawn_inputs(seed))
    spreads = {'L0_attn_a_D': (1.0, 0.2),
     'L0_attn_b_ln_q_g': (1.0, 0.2),
     'L0_attn_b_ln_q_b': (0.0, 0.1),
     'L0_attn_b_bq': (0.0, 0.1),
     'L0_attn_b_ln_kv_g': (1.0, 0.2),
     'L0_attn_b_ln_kv_b': (0.0, 0.1),
     'L0_attn_b_bkv': (0.0, 0.1),
     'L0_attn_b_ln_h_g': (1.0, 0.2),
     'L0_attn_b_ln_h_b': (0.0, 0.1),
     'L0_attn_b_bo': (0.0, 0.1),
     'L1_attn_a_q_a_ln_w': (1.0, 0.2),
     'L1_attn_a_kv_a_ln_w': (1.0, 0.2),
     'L1_attn_a_gate_b': (0.0, 0.1),
     'L1_attn_b_memory_norm': (1.0, 0.2)}
    factors = {'L0_attn_a_W_param': 8.0,
     'L0_attn_a_W_dt': 8.0,
     'L0_attn_a_b_dt': 8.0,
     'L0_attn_a_A_log': 8.0,
     'L1_attn_b_Wk': 3.968}
    for name, (base, spread) in spreads.items():
        noise = np.random.default_rng([zlib.crc32(name.encode()), seed]).standard_normal(out[name].shape)
        drawn = base * np.exp(spread * noise) if base else spread * noise
        out[name] = jnp.asarray(drawn.astype(out[name].dtype))
    for name, factor in factors.items():
        out[name] = (out[name] * factor).astype(out[name].dtype)
    return out
```

```python
from contextlib import ExitStack

import numpy as np

import concourse.bass as bass
from concourse import mybir

F32 = mybir.dt.float32
F32R = mybir.dt.float32r
U32 = mybir.dt.uint32
ALU = mybir.AluOpType
ACT = mybir.ActivationFunctionType
AX = mybir.AxisListType

P = 128
D = 256
KD = D // P
NB, L = 4, 512
T = NB * L
QT = L // P
LN_EPS, RMS_EPS = 1e-5, 1e-6

MH, MN, MK, MR = 32, 16, 4, 128
MI = MH * MN
MT = MI // P
E_ = (8, 16)
TOP = (2, 4)
I_ = (128, 176)
S_ = (256, 704)
NT = tuple((e * i + s + P - 1) // P for e, i, s in zip(E_, I_, S_))
GT = (5, 7)
TW = KD * 2 * P + D
AH, ANOPE, AROPE, AV, AQR, AKR = 16, 128, 64, 128, 192, 64
AQ = ANOPE + AROPE
HP = AH // 2
SH, SD = 16, 16
BQ, BH, BD = 4, 8, 8
START = 4000


class Count:

    def __init__(self, sem, table, name):
        self.sem, self.table, self.name = sem, table, name
        self.n, self.begin, self.loop = START, START, None

    def enter(self, loop):
        self.loop, self.begin = loop, self.n
        self.table[(self.name, "begin", loop)] = self.n

    def leave(self, rounds):
        per = self.n - self.begin
        self.table[(self.name, "per", self.loop)] = per
        self.n, self.loop = self.begin + rounds * per, None

    def step(self, what=None):
        self.n += 1
        if what is not None:
            self.table[(self.name, what)] = (self.n, self.loop)
        return 1

    def mark(self, what):
        self.table[(self.name, what)] = (self.n, self.loop)

    def per(self, loop):
        return self.table.get((self.name, "per", loop), 1)

    def at(self, what, b=0):
        n, loop = self.table.get((self.name, what), (START + 1, None))
        return n if loop is None else b * self.per(loop) + n

    def begun(self, loop, b):
        return b * self.per(loop) + self.table.get((self.name, "begin", loop), START)

    def last(self, b=0):
        return self.n if self.loop is None else b * self.per(self.loop) + self.n


class Layout:

    def __init__(self, *columns):
        self.at, self.n = {}, 0
        for name, k, n in columns:
            self.at[name] = (self.n, k, n)
            self.n += k * n

    def of(self, name, k=0, c0=0, c1=None):
        off, _, n = self.at[name]
        return slice(off + k * n + c0, off + k * n + (n if c1 is None else c1))

    def whole(self, name):
        off, k, n = self.at[name]
        return slice(off, off + k * n)

    def put(self, packed, name, array):
        off, k, n = self.at[name]
        array = np.asarray(array)
        assert array.shape[1] == n and array.shape[0] <= k * P, (name, array.shape)
        for j in range(k):
            rows = array[j * P:(j + 1) * P]
            packed[:rows.shape[0], off + j * n:off + (j + 1) * n] = rows


C_FFN = [Layout(("router", KD, E_[j] + j), ("iota", 1, QT * E_[j]), ("ident", 1, P)) for j in (0, 1)]
C_MAMBA = Layout(("conv_w", 1, MT * MK), ("conv_b", 1, MT), ("A_log", 1, MT), ("Dp", 1, MT), ("b_dt", 1, 1),
                 ("wdt", 1, MH))
C_ROT = Layout(("gq", 1, KD), ("bql", 1, KD), ("gkv", 1, KD), ("bkvl", 1, KD), ("bo", 1, KD), ("bqk", 1, 4),
               ("gh", 1, 1), ("bh", 1, 1), ("bv", 1, D), ("one_row", 1, 1), ("den", 1, P), ("cos", 1, L), ("sin", 1, L),
               ("cen", 1, P), ("cenp", 1, P), ("blk", 1, P))
C_GRP = Layout(("mem", 1, P), ("memn", 1, P), ("memw", 1, 1), ("one_row", 1, 1), ("den", 1, P))
C_PAT = Layout(("gatew", KD, 2 * P), ("gateb", 1, 2), ("one_row", 1, 1), ("den", 1, P))
C_LAT = Layout(("gatew", KD, 2 * P), ("gateb", 1, 2), ("qln", 1, 2), ("kvln", 1, 1), ("cos", 1, L), ("sin", 1, L),
               ("rot", 1, P), ("ident", 1, P))
M_LAT = Layout(("wqn", 1, AH * 2 * P), ("wkn", 1, AH * AKR), ("wvn", 1, AH * AKR), ("wot", 1, AH * D))
W_MAMBA = Layout(("wx", KD, MI), ("wz", KD, MI), ("wp", MT, MR + 2 * MI), ("wo", MT, D))
H_MAMBA = Layout(("expand", 1, MI))
W_PAT = Layout(("wq", KD, D), ("wk", KD, D), ("wv", KD, D), ("wo", 4, D))
H_PAT = Layout(("qh", 4, P), ("ql", 4, P), ("kh", 4, P), ("kl", 4, P), ("ident", 1, P))
W_LAT = Layout(("qa", KD, D), ("kva", KD, P), ("kpe", KD, HP * P), ("qpe", 2, HP * P))
W_GRP = Layout(("wq", KD, D), ("wk", KD, P), ("wv", KD, BH * BD))
H_GRP = Layout(("qh", 4, P), ("ql", 4, P), ("kh", 2, P), ("kl", 2, P), ("ident", 1, P), ("perm", 4, P))
W_ROT = Layout(("wq", KD, D), ("wk", KD, D), ("wv", KD, D), ("wo", 4, D))
H_ROT = Layout(("qh", 4, P), ("ql", 4, P), ("kh", 4, P), ("kl", 4, P), ("ident", 1, P))


def build(nc, io, out, plan, table):
    ctx = ExitStack()
    with ctx:
        def sb(name, shape, dt=F32):
            return ctx.enter_context(nc.sbuf_tensor(name, shape, dt))

        def sem(name):
            return ctx.enter_context(nc.semaphore(name))

        x = sb("x", [P, KD, T])
        c256 = sb("c256", [P, P])
        ones = sb("ones", [P, P])
        eps_ln = sb("eps_ln", [P, 1])
        eps_rms = sb("eps_rms", [P, 1])
        spare = sb("spare", [P, 1])
        NRAW, RAWW = 4, TW + P
        raw = sb("raw", [P, NRAW, RAWW])
        ps = [ctx.enter_context(nc.psum_tensor(f"ps{i}", [P, 2, L], F32)) for i in range(4)]
        bank = [ps[i // 2][:, i % 2, :] for i in range(8)]

        PE = Count(sem("tensor_done"), table, "PE")
        V = Count(sem("vector_done"), table, "V")
        A = Count(sem("scalar_done"), table, "A")
        G = Count(sem("gpsimd_done"), table, "G")
        raw_in = [sem(f"raw_in{i}") for i in range(NRAW)]
        kept, fetched, comp_in = sem("gated_pattern_kept"), sem("gated_pattern_fetched"), sem("composed_inputs_in")
        gated_pattern = nc.dram_tensor("gated_pattern", (P, KD, T), F32, kind="Internal").ap()
        x_in, c_in, stored = sem("x_in"), sem("c_in"), sem("stored")
        raws, c_loads = [0], [0]

        def stage_start(eng, s, params=True):
            if params:
                eng.wait_ge(c_in, 16 * (s + 1))
            if s:
                for other in (PE, V, A, G):
                    eng.wait_ge(other.sem, other.at(("end", s - 1)))

        def round_start(eng, loop, b):
            for other in (PE, V, A):
                eng.wait_ge(other.sem, other.begun(loop, b))

        def later(count, *whats):
            return max(whats, key=lambda what: table.get((count.name, what), (0, None))[0])

        def send_pieces(sp, pieces, first):
            for i, (src, n) in enumerate(pieces):
                p = first + i
                if p >= NRAW:
                    sp.wait_ge(G.sem, G.at(("cut", p - NRAW)))
                sp.dma_start(raw[:, p % NRAW, :n], src).then_inc(raw_in[p % NRAW], 16)

        def cut_pieces(pool, dests, first):
            for i, (nh, hi, nl, lo, before) in enumerate(dests):
                p = first + i
                for other, count in before:
                    pool.wait_ge(other.sem, count)
                pool.wait_ge(raw_in[p % NRAW], 16 * (p // NRAW + 1))
                nc.gpsimd.tensor_copy(hi, raw[:, p % NRAW, :nh]).then_inc(G.sem, G.step())
                pool.wait_ge(G.sem, G.last())
                if nl:
                    nc.gpsimd.tensor_tensor(lo, raw[:, p % NRAW, :nl], hi[:, 0:nl].bitcast(F32),
                                            ALU.subtract).then_inc(G.sem, G.step(("cut", p)))
                else:
                    nc.gpsimd.memset(spare[:, :], 0.0).then_inc(G.sem, G.step(("cut", p)))

        def mm3(psum, wh, wl, xh, xl, start, stop):
            nc.tensor.matmul(psum, wh, xh, start=start, stop=False)
            nc.tensor.matmul(psum, wh, xl, start=False, stop=False)
            return nc.tensor.matmul(psum, wl, xh, start=False, stop=stop)

        def ln_space(alloc):
            return (alloc("xb", [P, KD, L])[:, :, :], alloc("xc", [P, KD, L])[:, :, :],
                    alloc("sq", [P, KD, L])[:, :, :], alloc("dev", [P, L])[:, :])

        def ln_pe(pe, space, s, b, tag=""):
            xb, xc, sq, dev = space
            pe.wait_ge(V.sem, V.at((s, "x in" + tag), b))
            for k in range(KD):
                last = nc.tensor.matmul(bank[0], c256[:, :], xb[:, k, :], start=k == 0, stop=k == KD - 1)
            last.then_inc(PE.sem, PE.step((s, "mean" + tag)))
            pe.wait_ge(A.sem, A.at((s, "squared" + tag), b))
            for k in range(KD):
                last = nc.tensor.matmul(bank[1], c256[:, :], sq[:, k, :], start=k == 0, stop=k == KD - 1)
            last.then_inc(PE.sem, PE.step((s, "var" + tag)))

        def ln_act(act, space, s, b, tag=""):
            xb, xc, sq, dev = space
            act.wait_ge(V.sem, V.at((s, "centred" + tag), b))
            nc.scalar.activation(sq, xc, ACT.Square).then_inc(A.sem, A.step((s, "squared" + tag)))
            act.wait_ge(PE.sem, PE.at((s, "var" + tag), b))
            nc.scalar.activation(dev, bank[1], ACT.Sqrt, bias=eps_ln[:, :]).then_inc(A.sem, A.step((s, "dev" + tag)))

        def ln_vec(dve, space, s, b, tag="", load=True):
            xb, xc, sq, dev = space
            if load:
                nc.vector.tensor_copy(xb, x[:, :, bass.ts(b, L)]).then_inc(V.sem, V.step((s, "x in" + tag)))
            dve.wait_ge(V.sem, V.last(b))
            dve.wait_ge(PE.sem, PE.at((s, "mean" + tag), b))
            for k in range(KD):
                nc.vector.tensor_tensor(xc[:, k, :], xb[:, k, :], bank[0],
                                        ALU.subtract).then_inc(V.sem, V.step((s, "centred" + tag)))
            dve.wait_ge(V.sem, V.last(b))
            dve.wait_ge(A.sem, A.at((s, "dev" + tag), b))
            nc.vector.reciprocal(dev, dev).then_inc(V.sem, V.step())
            dve.wait_ge(V.sem, V.last(b))
            for k in range(KD):
                nc.vector.tensor_tensor(xb[:, k, :], xc[:, k, :], dev, ALU.mult).then_inc(V.sem, V.step((s, "xn" + tag)))

        counter = [0]

        def stage_memory():
            counter[0] += 1
            space, tag = ExitStack(), counter[0]

            def alloc(name, shape, dt=F32):
                return space.enter_context(nc.sbuf_tensor(f"{name}_{tag}", shape, dt))
            return space, alloc

        def weights(tag, lay, alloc, lo=True):
            hi = alloc(tag + "_hi", [P, lay.n], F32R)
            low = alloc(tag + "_lo", [P, lay.n], F32R) if lo else None
            cols = [(i, min(RAWW, lay.n - i)) for i in range(0, lay.n, RAWW)]
            pieces = [(io[tag][:, i:i + n], n) for i, n in cols]
            dests = [(n, hi[:, i:i + n], n if lo else 0, low[:, i:i + n] if lo else None, []) for i, n in cols]
            return hi, low, pieces, dests

        def stage_loads(name, c, pieces, dests):
            def sync(sp, s):
                stage_start(sp, s, params=False)
                sp.dma_start(c[:, :], io[f"c_{name}"]).then_inc(c_in, 16)
                send_pieces(sp, pieces, first[s])

            def pool(pool, s):
                stage_start(pool, s)
                cut_pieces(pool, dests, first[s])
            return sync, pool

        def mamba():
            C, W, H = C_MAMBA, W_MAMBA, H_MAMBA
            space, alloc = stage_memory()
            ln = ln_space(alloc)
            xb = ln[0]
            c = alloc("c", [P, C.n])
            WH, WL, p1, d1 = weights("w_mamba", W, alloc)
            EX, _, p2, d2 = weights("h_mamba", H, alloc, lo=False)
            sync, pool = stage_loads("mamba", c, p1 + p2, d1 + d2)
            npieces = len(p1) + len(p2)
            XH, XL = alloc("xn_hi", [P, KD, L], F32R), alloc("xn_lo", [P, KD, L], F32R)
            UH, UL = alloc("u_hi", [P, MT, L], F32R), alloc("u_lo", [P, MT, L], F32R)
            YH, YL = alloc("y_hi", [P, MT, L], F32R), alloc("y_lo", [P, MT, L], F32R)
            RH, RL = alloc("rank_hi", [P, L], F32R), alloc("rank_lo", [P, L], F32R)
            SHI, SLO = alloc("step_hi", [MH, L], F32R), alloc("step_lo", [MH, L], F32R)
            pad = alloc("padded", [P, MT, MK - 1 + L])
            cv = alloc("conv", [P, MT, L])
            u = alloc("u", [P, MT, L])
            ab = alloc("a_bar", [P, 2, L])
            du, bu, hs, y1 = (alloc(n, [P, L]) for n in ("du", "bu", "hs", "y1"))
            sp_ = alloc("softplus", [MH, 5, L])
            negA = alloc("neg_a", [P, MT])
            space.close()
            zs = cv

            def w(name, k, m):
                return WH[:, W.of(name, k, m * P, (m + 1) * P)], WL[:, W.of(name, k, m * P, (m + 1) * P)]

            Z_BANK = (6, 7, 0, 1)

            def pe(pe, s):
                def inner(name, m, bk, what):
                    for k in range(MT):
                        wh, wl = w(name, k, m)
                        last = mm3(bank[bk], wh, wl, UH[:, k, :], UL[:, k, :], k == 0, k == MT - 1)
                    last.then_inc(PE.sem, PE.step((s, what)))

                def B(m, b):
                    pe.wait_ge(A.sem, A.at((s, "z", m), b)) if m < 2 else pe.wait_ge(V.sem, V.at((s, "bu", m - 2), b))
                    inner("wp", 1 + m, 6 + m % 2, ("B", m))

                def Cc(m, b):
                    pe.wait_ge(A.sem, A.at((s, "z", 2 + m), b)) if m < 2 else pe.wait_ge(V.sem, V.at((s, "y1", m - 2), b))
                    inner("wp", 1 + MT + m, m % 2, ("C", m))

                def step(m, b):
                    pe.wait_ge(V.sem, V.at((s, "step lo"), b))
                    if m >= 2:
                        pe.wait_ge(V.sem, V.at((s, "du", m - 2), b))
                        pe.wait_ge(A.sem, A.at((s, "a bar", m - 2), b))
                    nc.tensor.matmul(bank[4 + m % 2], EX[0:MH, m * P:(m + 1) * P], SHI[:, :], start=True, stop=False)
                    nc.tensor.matmul(bank[4 + m % 2], EX[0:MH, m * P:(m + 1) * P], SLO[:, :],
                                     start=False, stop=True).then_inc(PE.sem, PE.step((s, "step", m)))

                pe.wait_ge(G.sem, G.at(("cut", first[s] + npieces - 1)))
                PE.enter(s)
                with pe.Fori(0, NB) as b:
                    round_start(pe, s, b)
                    ln_pe(pe, ln, s, b)
                    pe.wait_ge(V.sem, V.at((s, "xn lo"), b))
                    for name, banks in (("wx", (2, 3, 4, 5)), ("wz", Z_BANK)):
                        for m in range(MT):
                            for k in range(KD):
                                wh, wl = w(name, k, m)
                                last = mm3(bank[banks[m]], wh, wl, XH[:, k, :], XL[:, k, :], k == 0, k == KD - 1)
                            last.then_inc(PE.sem, PE.step((s, name, m)))
                    pe.wait_ge(V.sem, V.at((s, "u lo"), b))
                    inner("wp", 0, 2, "rank")
                    B(0, b)
                    pe.wait_ge(V.sem, V.at((s, "rank"), b))
                    nc.tensor.matmul(bank[3][0:MH, :], c[:, C.whole("wdt")], y1[:, :],
                                     start=True, stop=True).then_inc(PE.sem, PE.step((s, "steps")))
                    Cc(0, b)
                    B(1, b)
                    Cc(1, b)
                    step(0, b)
                    step(1, b)
                    for m in (2, 3):
                        B(m, b)
                        Cc(m, b)
                        step(m, b)
                    for k in range(MT):
                        pe.wait_ge(V.sem, V.at((s, "y lo", k), b))
                        for m in range(KD):
                            wh, wl = w("wo", k, m)
                            last = mm3(bank[2 + m], wh, wl, YH[:, k, :], YL[:, k, :], k == 0, k == MT - 1)
                    last.then_inc(PE.sem, PE.step((s, "out")))
                PE.leave(NB)

            def act(act, s):
                nc.scalar.activation(negA[:, :], c[:, C.whole("A_log")], ACT.Exp).then_inc(A.sem, A.step((s, "exp A")))
                A.enter(s)
                with act.Fori(0, NB) as b:
                    round_start(act, s, b)
                    ln_act(act, ln, s, b)
                    for m in range(MT):
                        act.wait_ge(PE.sem, PE.at((s, "wx", m), b))
                        nc.scalar.activation(pad[:, m, MK - 1:], bank[2 + m], ACT.Copy).then_inc(A.sem, A.step((s, "x", m)))
                    for m in range(MT):
                        act.wait_ge(V.sem, V.at((s, "conv", m), b))
                        nc.scalar.activation(u[:, m, :], cv[:, m, :], ACT.Silu).then_inc(A.sem, A.step((s, "u", m)))
                    for m in range(MT):
                        act.wait_ge(PE.sem, PE.at((s, "wz", m), b))
                        act.wait_ge(A.sem, A.last(b))
                        nc.scalar.activation(zs[:, m, :], bank[Z_BANK[m]], ACT.Silu).then_inc(A.sem, A.step((s, "z", m)))
                    act.wait_ge(PE.sem, PE.at((s, "steps"), b))
                    nc.scalar.activation(sp_[:, 0, :], bank[3][0:MH, :], ACT.Abs,
                                         bias=c[0:MH, C.whole("b_dt")]).then_inc(A.sem, A.step())
                    act.wait_ge(A.sem, A.last(b))
                    nc.scalar.activation(sp_[:, 1, :], sp_[:, 0, :], ACT.Exp, scale=-1.0).then_inc(A.sem, A.step((s, "e")))
                    act.wait_ge(V.sem, V.at((s, "1 + e"), b))
                    nc.scalar.activation(sp_[:, 3, :], sp_[:, 2, :], ACT.Ln).then_inc(A.sem, A.step((s, "log")))
                    for m in range(MT):
                        act.wait_ge(PE.sem, PE.at((s, "step", m), b))
                        if m >= 2:
                            act.wait_ge(V.sem, V.at((s, "scan", m - 2), b))
                        nc.scalar.activation(ab[:, m % 2, :], bank[4 + m % 2], ACT.Exp,
                                             scale=negA[:, m:m + 1]).then_inc(A.sem, A.step((s, "a bar", m)))
                A.leave(NB)

            def vec(dve, s):
                nc.vector.memset(pad[:, :, 0:MK - 1], 0.0).then_inc(V.sem, V.step())
                dve.wait_ge(A.sem, A.at((s, "exp A")))
                nc.vector.tensor_scalar(negA[:, :], negA[:, :], -1.0, None, ALU.mult).then_inc(V.sem, V.step())
                V.enter(s)
                with dve.Fori(0, NB) as b:
                    def after_last():
                        dve.wait_ge(V.sem, V.last(b))

                    round_start(dve, s, b)
                    ln_vec(dve, ln, s, b)
                    after_last()
                    nc.vector.tensor_copy(XH[:, :, :], xb).then_inc(V.sem, V.step())
                    after_last()
                    nc.vector.tensor_tensor(XL[:, :, :], xb, XH[:, :, :].bitcast(F32), ALU.subtract).then_inc(V.sem, V.step((s, "xn lo")))
                    for m in range(MT):
                        dve.wait_ge(A.sem, A.at((s, "x", m), b))
                        nc.vector.tensor_scalar(cv[:, m, :], pad[:, m, 0:L], c[:, C.of("conv_w", 0, m * MK, m * MK + 1)],
                                                c[:, C.of("conv_b", 0, m, m + 1)], ALU.mult, ALU.add).then_inc(V.sem, V.step())
                        for k in range(1, MK):
                            after_last()
                            nc.vector.scalar_tensor_tensor(cv[:, m, :], pad[:, m, k:k + L], c[:, C.of("conv_w", 0, m * MK + k, m * MK + k + 1)],
                                                           cv[:, m, :], ALU.mult, ALU.add).then_inc(V.sem, V.step((s, "conv", m)))
                    for m in range(MT):
                        dve.wait_ge(A.sem, A.at((s, "u", m), b))
                        nc.vector.tensor_copy(UH[:, m, :], u[:, m, :]).then_inc(V.sem, V.step())
                        after_last()
                        nc.vector.tensor_tensor(UL[:, m, :], u[:, m, :], UH[:, m, :].bitcast(F32),
                                                ALU.subtract).then_inc(V.sem, V.step((s, "u lo")))
                    dve.wait_ge(PE.sem, PE.at((s, "rank"), b))
                    nc.vector.tensor_copy(y1[:, :], bank[2]).then_inc(V.sem, V.step((s, "rank")))
                    dve.wait_ge(A.sem, A.at((s, "e"), b))
                    nc.vector.tensor_scalar(sp_[:, 2, :], sp_[:, 1, :], 1.0, None, ALU.add).then_inc(V.sem, V.step((s, "1 + e")))
                    after_last()
                    nc.vector.scalar_tensor_tensor(sp_[:, 4, :], sp_[:, 2, :], -1.0, sp_[:, 1, :], ALU.add,
                                                   ALU.subtract).then_inc(V.sem, V.step())
                    dve.wait_ge(A.sem, A.at((s, "log"), b))
                    after_last()
                    nc.vector.tensor_tensor(sp_[:, 3, :], sp_[:, 3, :], sp_[:, 4, :], ALU.subtract).then_inc(V.sem, V.step())
                    nc.vector.tensor_scalar(sp_[:, 0, :], bank[3][0:MH, :], c[0:MH, C.whole("b_dt")], 0.0, ALU.add,
                                            ALU.max).then_inc(V.sem, V.step())
                    after_last()
                    nc.vector.tensor_tensor(sp_[:, 3, :], sp_[:, 3, :], sp_[:, 0, :], ALU.add).then_inc(V.sem, V.step())
                    after_last()
                    nc.vector.tensor_copy(SHI[:, :], sp_[:, 3, :]).then_inc(V.sem, V.step())
                    after_last()
                    nc.vector.tensor_tensor(SLO[:, :], sp_[:, 3, :], SHI[:, :].bitcast(F32),
                                            ALU.subtract).then_inc(V.sem, V.step((s, "step lo")))
                    for m in range(MT):
                        dve.wait_ge(PE.sem, PE.at((s, "step", m), b))
                        dve.wait_ge(A.sem, A.at((s, "a bar", m), b))
                        after_last()
                        nc.vector.tensor_tensor(du[:, :], u[:, m, :], bank[4 + m % 2], ALU.mult).then_inc(V.sem, V.step((s, "du", m)))
                        dve.wait_ge(PE.sem, PE.at((s, ("B", m)), b))
                        after_last()
                        nc.vector.tensor_tensor(bu[:, :], du[:, :], bank[6 + m % 2], ALU.mult).then_inc(V.sem, V.step((s, "bu", m)))
                        after_last()
                        nc.vector.tensor_tensor_scan(hs[:, :], ab[:, m % 2, :], bu[:, :], 0.0, ALU.mult,
                                                     ALU.add).then_inc(V.sem, V.step((s, "scan", m)))
                        dve.wait_ge(PE.sem, PE.at((s, ("C", m)), b))
                        after_last()
                        nc.vector.tensor_tensor(y1[:, :], hs[:, :], bank[m % 2], ALU.mult).then_inc(V.sem, V.step((s, "y1", m)))
                        after_last()
                        nc.vector.scalar_tensor_tensor(y1[:, :], u[:, m, :], c[:, C.of("Dp", 0, m, m + 1)], y1[:, :],
                                                       ALU.mult, ALU.add).then_inc(V.sem, V.step())
                        after_last()
                        nc.vector.tensor_tensor(y1[:, :], y1[:, :], zs[:, m, :], ALU.mult).then_inc(V.sem, V.step())
                        after_last()
                        nc.vector.tensor_copy(YH[:, m, :], y1[:, :]).then_inc(V.sem, V.step())
                        after_last()
                        nc.vector.tensor_tensor(YL[:, m, :], y1[:, :], YH[:, m, :].bitcast(F32),
                                                ALU.subtract).then_inc(V.sem, V.step((s, "y lo", m)))
                    dve.wait_ge(PE.sem, PE.at((s, "out"), b))
                    nc.vector.tensor_tensor(x[:, :, bass.ts(b, L)], x[:, :, bass.ts(b, L)], ps[1][:, :, :],
                                            ALU.add).then_inc(V.sem, V.step())
                V.leave(NB)

            return {"sync": sync, "pool": pool, "pe": pe, "act": act, "vec": vec, "pieces": npieces}


        def ffn(j):
            E, top, nt, gt = E_[j], TOP[j], NT[j], GT[j]
            NE = E + j
            NR = nt if j else E * I_[j] // P
            NG = nt // gt
            rounds = NG // 2
            C = C_FFN[j]
            space, alloc = stage_memory()
            ln = ln_space(alloc)
            xb = ln[0]
            c = alloc("c", [P, C.n])
            XH = alloc("xn_hi", [P, KD, T], F32R)
            XL = alloc("xn_lo", [P, KD, T], F32R)
            CT = alloc("combine", [P, T], F32R)
            WH = alloc("w_hi", [P, 2, gt, TW + P], F32R)
            WL = alloc("w_lo", [P, 2, gt, TW], F32R)
            HH = alloc("h_hi", [P, 3, L], F32R)
            HL = alloc("h_lo", [P, 3, L], F32R)
            NC = 2 * NE if j else 2 * E
            CP = P if j else 32
            lg = alloc("logits", [P, QT, NE])[:, :, :]
            pr = alloc("probs", [P, QT, E])[:, :, :]
            mask = alloc("mask", [P, QT, E])[:, :, :]
            eq = alloc("eq", [P, QT, E])[:, :, :]
            cw = alloc("cw", [P, QT, CP])[:, :, :]
            cwr = alloc("cw_whole", [P, QT, NE])[:, :, :]
            st = alloc("gate_exp", [P, QT])[:, :]
            top8 = alloc("top8", [P, QT, 8])[:, :, :]
            idx = alloc("idx", [P, QT, 8], U32)
            idf = alloc("idf", [P, QT, 8])[:, :, :]
            dummy = alloc("dummy", [P, 1])[:, :]
            sg = alloc("silu", [P, 2, L])[:, :, :]
            ga = alloc("gated", [P, L])[:, :]
            hb = alloc("h", [P, L])[:, :]
            space.close()
            iota = c[:, C.whole("iota")].rearrange("p (q e) -> p q e", q=QT)
            seq = [(par, ch, t) for par in (0, 1) for ch in range(NB) for t in range(gt)]

            def wp(par, t, k, part):
                o = KD * 2 * P + k * P if part == "down" else (k * 2 + (part == "up")) * P
                return WH[:, par, t, o:o + P], WL[:, par, t, o:o + P]

            def sync(sp, s):
                stage_start(sp, s, params=False)
                sp.dma_start(c[:, :], io[f"c_ffn{j}"]).then_inc(c_in, 16)
                send_pieces(sp, [(io[f"w_ffn{j}"][t], TW + P) for t in range(nt)], first[s])

            def pool(pool, s):
                stage_start(pool, s)
                dests = []
                for t in range(nt):
                    g, i = divmod(t, gt)
                    before = [(PE, PE.at((s, "group read", g % 2), g // 2 - 1))] if g >= 2 and i == 0 else []
                    dests.append((TW + P, WH[:, g % 2, i, :], TW, WL[:, g % 2, i, :], before))
                cut_pieces(pool, dests, first[s])

            def pe(pe, s):
                PE.enter((s, "route"))
                with pe.Fori(0, NB) as b:
                    round_start(pe, (s, "route"), b)
                    ln_pe(pe, ln, s, b)
                    pe.wait_ge(V.sem, V.at((s, "xn"), b))
                    for q in range(QT):
                        for k in range(KD):
                            last = nc.tensor.matmul(bank[2][:, q * NE:(q + 1) * NE], xb[:, k, q * P:(q + 1) * P],
                                                    c[:, C.of("router", k)], start=k == 0, stop=k == KD - 1)
                    last.then_inc(PE.sem, PE.step((s, "logits")))
                    pe.wait_ge(V.sem, V.at((s, "combine"), b))
                    for q in range(QT):
                        last = nc.tensor.transpose(bank[3][0:CP, q * P:(q + 1) * P], cw[:, q, :],
                                                   c[:, C.whole("ident")])
                    last.then_inc(PE.sem, PE.step((s, "combine turned")))
                PE.leave(NB)

                def up(i, b):
                    par, ch, t = seq[i]
                    if ch == 0:
                        pe.wait_ge(G.sem, G.at(("cut", wfirst + par * gt + t)) + b * 4 * gt)
                    if i >= 2:
                        pe.wait_ge(A.sem, A.at((s, "silu", i - 2), b))
                        pe.wait_ge(V.sem, V.at((s, "gated", i - 2), b))
                    for part, bk in (("gate", i % 2), ("up", 2 + i % 2)):
                        for k in range(KD):
                            wh, wl = wp(par, t, k, part)
                            last = mm3(bank[bk], wh, wl, XH[:, k, ch * L:(ch + 1) * L],
                                       XL[:, k, ch * L:(ch + 1) * L], k == 0, k == KD - 1)
                        last.then_inc(PE.sem, PE.step((s, part, i)))
                    if par * gt + t < NR:
                        if i >= 2:
                            pe.wait_ge(V.sem, V.at((s, "h", i - 2), b))
                        nc.tensor.matmul(bank[4 + i % 2], WH[0:NC, par, t, TW:TW + P], CT[0:NC, ch * L:(ch + 1) * L],
                                         start=True, stop=True).then_inc(PE.sem, PE.step((s, "weights", i)))

                def down(i, b):
                    par, ch, t = seq[i]
                    pe.wait_ge(V.sem, V.at((s, "h lo", i), b))
                    if t == 0 and i >= gt:
                        pe.wait_ge(V.sem, V.at((s, "added", i - 1), b))
                    for m in range(KD):
                        wh, wl = wp(par, t, m, "down")
                        last = mm3(bank[6 + m], wh, wl, HH[:, i % 3, :], HL[:, i % 3, :], t == 0, t == gt - 1)
                    last.then_inc(PE.sem, PE.step((s, "down", i)))
                    if ch == NB - 1 and t == gt - 1:
                        PE.mark((s, "group read", par))

                wfirst = first[s]

                def body(b):
                    round_start(pe, (s, "experts"), b)
                    for i in range(len(seq) + 2):
                        if i < len(seq):
                            up(i, b)
                        if i >= 2:
                            down(i - 2, b)

                PE.enter((s, "experts"))
                if rounds > 1:
                    with pe.Fori(0, rounds) as b:
                        body(b)
                else:
                    body(0)
                PE.leave(rounds)

            def act(act, s):
                A.enter((s, "route"))
                with act.Fori(0, NB) as b:
                    round_start(act, (s, "route"), b)
                    ln_act(act, ln, s, b)
                    act.wait_ge(V.sem, V.at((s, "shifted"), b))
                    nc.scalar.activation(pr, lg[:, :, 0:E], ACT.Exp).then_inc(A.sem, A.step((s, "exp")))
                    if j:
                        act.wait_ge(PE.sem, PE.at((s, "logits"), b))
                        lgp = bank[2][:, 0:QT * NE].rearrange("p (q e) -> p q e", q=QT)
                        nc.scalar.activation(st, lgp[:, :, E], ACT.Exp, scale=-1.0).then_inc(A.sem, A.step((s, "exp gate")))
                A.leave(NB)

                def body(b):
                    round_start(act, (s, "experts"), b)
                    for i in range(len(seq)):
                        act.wait_ge(PE.sem, PE.at((s, "gate", i), b))
                        if i >= 2:
                            act.wait_ge(V.sem, V.at((s, "gated", i - 2), b))
                        nc.scalar.activation(sg[:, i % 2, :], bank[i % 2], ACT.Silu).then_inc(A.sem, A.step((s, "silu", i)))

                A.enter((s, "experts"))
                if rounds > 1:
                    with act.Fori(0, rounds) as b:
                        body(b)
                else:
                    body(0)
                A.leave(rounds)

            def vec(dve, s):
                V.enter((s, "route"))
                with dve.Fori(0, NB) as b:
                    def after_last():
                        dve.wait_ge(V.sem, V.last(b))

                    round_start(dve, (s, "route"), b)
                    ln_vec(dve, ln, s, b)
                    after_last()
                    nc.vector.tensor_copy(XH[:, :, bass.ts(b, L)], xb).then_inc(V.sem, V.step())
                    after_last()
                    nc.vector.tensor_tensor(XL[:, :, bass.ts(b, L)], xb, XH[:, :, bass.ts(b, L)].bitcast(F32),
                                            ALU.subtract).then_inc(V.sem, V.step())
                    dve.wait_ge(PE.sem, PE.at((s, "logits"), b))
                    lgp = bank[2][:, 0:QT * NE].rearrange("p (q e) -> p q e", q=QT)
                    nc.vector.tensor_reduce(idf[:, :, 0], lgp[:, :, 0:E], op=ALU.max, axis=AX.X).then_inc(V.sem, V.step())
                    after_last()
                    nc.vector.tensor_tensor(lg[:, :, 0:E], lgp[:, :, 0:E], idf[:, :, 0:1].to_broadcast([P, QT, E]),
                                            ALU.subtract).then_inc(V.sem, V.step((s, "shifted")))
                    dve.wait_ge(A.sem, A.at((s, "exp"), b))
                    nc.vector.tensor_reduce(idf[:, :, 1], pr, op=ALU.add, axis=AX.X).then_inc(V.sem, V.step())
                    after_last()
                    nc.vector.reciprocal(idf[:, :, 2], idf[:, :, 1]).then_inc(V.sem, V.step())
                    after_last()
                    nc.vector.tensor_tensor(pr, pr, idf[:, :, 2:3].to_broadcast([P, QT, E]), ALU.mult).then_inc(V.sem, V.step())
                    for q in range(QT):
                        dve.wait_ge(V.sem, V.last(b))
                        nc.vector.memset(dummy, 0.0).then_inc(V.sem, V.step())
                        nc.vector.max(top8[:, q, :], pr[:, q, :]).then_inc(V.sem, V.step())
                    for q in range(QT):
                        dve.wait_ge(V.sem, V.last(b))
                        nc.vector.memset(dummy, 0.0).then_inc(V.sem, V.step())
                        nc.vector.max_index(idx[:, q, :], top8[:, q, :], pr[:, q, :]).then_inc(V.sem, V.step())
                    after_last()
                    nc.vector.tensor_copy(idf, idx[:, :, :]).then_inc(V.sem, V.step())
                    for k in range(top):
                        after_last()
                        nc.vector.tensor_tensor(eq if k else mask, iota, idf[:, :, k:k + 1].to_broadcast([P, QT, E]),
                                                ALU.is_equal).then_inc(V.sem, V.step())
                        if k:
                            after_last()
                            nc.vector.tensor_tensor(mask, mask, eq, ALU.add).then_inc(V.sem, V.step())
                    after_last()
                    nc.vector.tensor_tensor(mask, mask, pr, ALU.mult).then_inc(V.sem, V.step())
                    after_last()
                    nc.vector.tensor_reduce(idf[:, :, 1], mask, op=ALU.add, axis=AX.X).then_inc(V.sem, V.step())
                    after_last()
                    nc.vector.reciprocal(idf[:, :, 2], idf[:, :, 1]).then_inc(V.sem, V.step())
                    after_last()
                    nc.vector.tensor_tensor(cwr[:, :, 0:E], mask, idf[:, :, 2:3].to_broadcast([P, QT, E]),
                                            ALU.mult).then_inc(V.sem, V.step())
                    if j:
                        dve.wait_ge(A.sem, A.at((s, "exp gate"), b))
                        nc.vector.tensor_scalar(idf[:, :, 3], st, 1.0, None, ALU.add).then_inc(V.sem, V.step())
                        after_last()
                        nc.vector.reciprocal(cwr[:, :, E], idf[:, :, 3]).then_inc(V.sem, V.step())
                    after_last()
                    nc.vector.memset(cw, 0.0).then_inc(V.sem, V.step())
                    after_last()
                    nc.vector.tensor_copy(cw[:, :, 0:NE].bitcast(F32R), cwr[:, :, 0:NE]).then_inc(V.sem, V.step())
                    after_last()
                    nc.vector.tensor_tensor(cw[:, :, NE:2 * NE], cwr[:, :, 0:NE], cw[:, :, 0:NE],
                                            ALU.subtract).then_inc(V.sem, V.step((s, "combine")))
                    dve.wait_ge(PE.sem, PE.at((s, "combine turned"), b))
                    nc.vector.tensor_copy(CT[0:CP, bass.ts(b, L)], bank[3][0:CP, :]).then_inc(V.sem, V.step())
                V.leave(NB)

                def body(b):
                    def after_last():
                        dve.wait_ge(V.sem, V.last(b))

                    round_start(dve, (s, "experts"), b)
                    for i in range(len(seq) + 2):
                        if i < len(seq):
                            par, ch, t = seq[i]
                            routed = par * gt + t < NR
                            dve.wait_ge(A.sem, A.at((s, "silu", i), b))
                            dve.wait_ge(PE.sem, PE.at((s, "up", i), b))
                            after_last()
                            nc.vector.tensor_tensor(ga if routed else hb, sg[:, i % 2, :], bank[2 + i % 2],
                                                    ALU.mult).then_inc(V.sem, V.step((s, "gated", i)))
                            after_last()
                            if routed:
                                dve.wait_ge(PE.sem, PE.at((s, "weights", i), b))
                                nc.vector.tensor_tensor(hb, ga, bank[4 + i % 2], ALU.mult).then_inc(V.sem, V.step((s, "h", i)))
                                after_last()
                            else:
                                V.mark((s, "h", i))
                            if i >= 3:
                                dve.wait_ge(PE.sem, PE.at((s, "down", i - 3), b))
                            nc.vector.tensor_copy(HH[:, i % 3, :], hb).then_inc(V.sem, V.step())
                            after_last()
                            nc.vector.tensor_tensor(HL[:, i % 3, :], hb, HH[:, i % 3, :].bitcast(F32),
                                                    ALU.subtract).then_inc(V.sem, V.step((s, "h lo", i)))
                        if i >= 2 and seq[i - 2][2] == gt - 1:
                            ch = seq[i - 2][1]
                            dve.wait_ge(PE.sem, PE.at((s, "down", i - 2), b))
                            after_last()
                            nc.vector.tensor_tensor(x[:, :, ch * L:(ch + 1) * L], x[:, :, ch * L:(ch + 1) * L],
                                                    ps[3][:, :, :], ALU.add).then_inc(V.sem, V.step((s, "added", i - 2)))

                V.enter((s, "experts"))
                if rounds > 1:
                    with dve.Fori(0, rounds) as b:
                        body(b)
                else:
                    body(0)
                V.leave(rounds)

            return {"sync": sync, "pool": pool, "pe": pe, "act": act, "vec": vec, "pieces": nt}

        AUXB = (4, 5, 7)

        def small_heads(alloc, tag, heads, width, rows, khead, scale, q_tile, k_tile, k_tiles, c, C, S, SEL):
            per = P // rows
            G4 = heads // 4
            tiles = 4 // per
            shared = k_tiles < G4 * tiles
            bias_row = 3 * width
            nkv = len({khead(h) for h in range(heads)})
            QS = alloc("q_stack", [P, 2, tiles, L], F32R)
            KS = alloc("k_stack", [P, k_tiles if shared else 2 * tiles, L], F32R)
            MB = alloc("max_cols", [P, 2, QT, P], F32R)
            VA = alloc("v_aug", [P, QT, nkv, 32])
            PB = alloc("probs", [P, 4, 2, L])
            OS = alloc("o_sums", [P, 2, L])
            REC = alloc("o_recip", [P, L])
            OH, OL = alloc("o_hi", [P, G4, L], F32R), alloc("o_lo", [P, G4, L], F32R)

            def kslot(t):
                return t % k_tiles if shared else t % (2 * tiles)

            def group_aux(g):
                ev = []
                for t in range(g * tiles, (g + 1) * tiles):
                    if not shared:
                        ev.append(("ek", t))
                    ev.append(("eq", t))
                for t in range(g * tiles, (g + 1) * tiles):
                    ev += [("mx", t * per + i, q) for i in range(per) for q in range(QT)]
                    ev.append(("bias", t))
                return ev

            units = [(g, kt) for g in range(G4) for kt in range(QT)]
            events = [("v", q) for q in range(QT)] + ([("ek", t) for t in range(k_tiles)] if shared else []) + group_aux(0)
            aux = []
            for n in range(len(units) + 1):
                if n < len(units):
                    g, kt = units[n]
                    if kt == 0:
                        aux += group_aux(g + 1) if g + 1 < G4 else []
                        share = -(-len(aux) // (2 * QT)) if aux else 0
                    for pair in (0, 1):
                        events.append(("s", g, kt, pair))
                        for _ in range(min(share, len(aux))):
                            events.append(aux.pop(0))
                    if kt == QT - 1:
                        events += aux
                        aux = []
                if n:
                    g, kt = units[n - 1]
                    events.append(("pv", g, kt))
                    if kt == QT - 1:
                        events.append(("sums", g))
                    if kt == 1 and g:
                        events.append(("norm", g - 1))
            events.append(("norm", G4 - 1))
            reader = {"v": A, "ek": A, "eq": A, "mx": V, "bias": V, "norm": V}
            aux_no, order = {}, []
            for ev in events:
                if ev[0] in reader:
                    aux_no[ev] = len(order)
                    order.append(ev)

            def slot(ev):
                return AUXB[aux_no[ev] % 3]

            def step_no(g, kt, pair):
                return (g * QT + kt) * 2 + pair

            def pe(pe, s, b, value_product):
                for ev in events:
                    kind = ev[0]
                    by_act, by_vec = [], []
                    if kind in reader and aux_no[ev] >= 3:
                        old = order[aux_no[ev] - 3]
                        (by_act if reader[old[0]] is A else by_vec).append((s, tag, old))
                    if kind == "mx" and ev[2] == 0 and ev[1] % per == 0:
                        by_act.append((s, tag, ("eq", ev[1] // per)))
                    if kind == "bias":
                        by_vec.append((s, tag, ("mx", ev[1] * per + per - 1, QT - 1)))
                    if kind == "s":
                        n = step_no(*ev[1:])
                        if ev[2] == 0:
                            by_vec.append((s, tag, ("bias", (ev[1] * 4 + ev[3] * 2) // per)))
                        if n >= 2:
                            by_act.append((s, tag, "exp", n - 2))
                    if kind == "pv":
                        by_act.append((s, tag, "exp", step_no(*ev[1:], 1)))
                        if ev[2] == 0 and ev[1]:
                            by_act.append((s, tag, ("sums", ev[1] - 1)))
                    if kind == "norm":
                        by_act.append((s, tag, ("sums", ev[1])))
                    if by_act:
                        pe.wait_ge(A.sem, A.at(later(A, *by_act), b))
                    if by_vec:
                        pe.wait_ge(V.sem, V.at(later(V, *by_vec), b))
                    if kind == "v":
                        value_product(bank[slot(ev)], ev[1])
                        last = None
                    elif kind in ("ek", "eq"):
                        ct, pat = (k_tile if kind == "ek" else q_tile)(ev[1])
                        hi, lo, rows_in = (ct if isinstance(ct, tuple) else ct)
                        sel = SEL["k" if kind == "ek" else "q"]
                        nc.tensor.matmul(bank[slot(ev)], sel[0](pat), hi, start=True, stop=False)
                        last = nc.tensor.matmul(bank[slot(ev)], sel[1](pat), lo, start=False, stop=True)
                        last.then_inc(PE.sem, PE.step((s, tag, ev)))
                    elif kind == "mx":
                        h, q = ev[1:]
                        t, r = h // per, (h % per) * rows
                        g = t // tiles
                        nc.tensor.matmul(bank[slot(ev)], QS[r:r + rows, g % 2, t % tiles, q * P:(q + 1) * P],
                                         KS[r:r + rows, kslot(t), :], start=True,
                                         stop=True).then_inc(PE.sem, PE.step((s, tag, ev)))
                    elif kind == "bias":
                        t = ev[1]
                        for q in range(QT):
                            last = nc.tensor.matmul(bank[slot(ev)][:, q * P:(q + 1) * P], MB[:, t % 2, q, :],
                                                    SEL["ident"], start=True, stop=True)
                        last.then_inc(PE.sem, PE.step((s, tag, ev)))
                    elif kind == "s":
                        g, kt, pair = ev[1:]
                        n = step_no(g, kt, pair)
                        for i in (0, 1):
                            h = g * 4 + pair * 2 + i
                            t, r = h // per, (h % per) * rows
                            last = nc.tensor.matmul(ps[n % 2][:, i, :], KS[r:r + rows, kslot(t), kt * P:(kt + 1) * P],
                                                    QS[r:r + rows, g % 2, t % tiles, :], start=True, stop=True)
                        last.then_inc(PE.sem, PE.step((s, tag, ev)))
                    elif kind == "pv":
                        g, kt = ev[1:]
                        for i in range(4):
                            n = step_no(g, kt, i // 2)
                            last = nc.tensor.matmul(bank[6][32 * i:32 * i + 32, :], VA[:, kt, khead(g * 4 + i), :],
                                                    PB[:, n % 4, i % 2, :], start=kt == 0, stop=kt == QT - 1)
                        last.then_inc(PE.sem, PE.step((s, tag, ev)))
                    elif kind == "norm":
                        g = ev[1]
                        nc.tensor.matmul(bank[slot(ev)], c[:, C.whole("den")], OS[:, g % 2, :], start=True,
                                         stop=True).then_inc(PE.sem, PE.step((s, tag, ev)))

            def act(act, s, b):
                for ev in events:
                    kind = ev[0]
                    if kind == "v":
                        act.wait_ge(PE.sem, PE.at((s, tag, ev), b))
                        nc.scalar.activation(VA[:, ev[1], :, 0:width],
                                             bank[slot(ev)][:, 0:nkv * width].rearrange("p (h d) -> p h d", d=width),
                                             ACT.Copy).then_inc(A.sem, A.step((s, tag, ev)))
                    elif kind in ("ek", "eq"):
                        t = ev[1]
                        g = t // tiles
                        act.wait_ge(PE.sem, PE.at((s, tag, ev), b))
                        if kind == "eq":
                            nc.scalar.activation(QS[:, g % 2, t % tiles, :], bank[slot(ev)],
                                                 ACT.Copy).then_inc(A.sem, A.step((s, tag, ev)))
                        else:
                            nc.scalar.activation(KS[:, kslot(t), :], bank[slot(ev)], ACT.Identity,
                                                 bias=c[:, C.whole("one_row")]).then_inc(A.sem, A.step((s, tag, ev)))
                    elif kind == "s":
                        g, kt, pair = ev[1:]
                        n = step_no(g, kt, pair)
                        act.wait_ge(PE.sem, PE.at((s, tag, ev), b))
                        nc.scalar.activation(PB[:, n % 4, :, :], ps[n % 2][:, :, :], ACT.Exp,
                                             scale=scale).then_inc(A.sem, A.step((s, tag, "exp", n)))
                    elif kind == "sums":
                        g = ev[1]
                        act.wait_ge(PE.sem, PE.at((s, tag, ("pv", g, QT - 1)), b))
                        if g >= 2:
                            act.wait_ge(V.sem, V.at((s, tag, "scaled", g - 2), b))
                        nc.scalar.activation(OS[:, g % 2, :], bank[6], ACT.Copy).then_inc(A.sem, A.step((s, tag, ev)))

            def vec(dve, s, b):
                for ev in events:
                    kind = ev[0]
                    if kind == "mx":
                        h, q = ev[1:]
                        t = h // per
                        col = (h % per) * rows + bias_row
                        dve.wait_ge(PE.sem, PE.at((s, tag, ev), b))
                        nc.vector.tensor_reduce(MB[:, t % 2, q, col:col + 1], bank[slot(ev)], op=ALU.max, axis=AX.X,
                                                negate=True).then_inc(V.sem, V.step((s, tag, ev)))
                    elif kind == "bias":
                        t = ev[1]
                        q = QS[:, (t // tiles) % 2, t % tiles, :]
                        dve.wait_ge(PE.sem, PE.at((s, tag, ev), b))
                        nc.vector.tensor_tensor(q, q.bitcast(F32), bank[slot(ev)], ALU.add).then_inc(V.sem, V.step((s, tag, ev)))
                    elif kind == "norm":
                        g = ev[1]
                        dve.wait_ge(PE.sem, PE.at((s, tag, ev), b))
                        dve.wait_ge(V.sem, V.last(b))
                        nc.vector.reciprocal(REC[:, :], bank[slot(ev)]).then_inc(V.sem, V.step((s, tag, ev)))
                        dve.wait_ge(V.sem, V.last(b))
                        nc.vector.tensor_tensor(REC[:, :], OS[:, g % 2, :], REC[:, :], ALU.mult).then_inc(V.sem, V.step((s, tag, "scaled", g)))
                        dve.wait_ge(V.sem, V.last(b))
                        nc.vector.tensor_copy(OH[:, g, :], REC[:, :]).then_inc(V.sem, V.step())
                        dve.wait_ge(V.sem, V.last(b))
                        nc.vector.tensor_tensor(OL[:, g, :], REC[:, :], OH[:, g, :].bitcast(F32),
                                                ALU.subtract).then_inc(V.sem, V.step((s, tag, "o", g)))

            def vec_begin():
                nc.vector.memset(MB[:, :, :, :].bitcast(F32), 0.0).then_inc(V.sem, V.step())
                nc.vector.memset(VA[:, :, :, :], 0.0).then_inc(V.sem, V.step())

            def vec_ones(dve):
                dve.wait_ge(V.sem, V.last())
                nc.vector.memset(VA[:, :, :, width:width + 1], 1.0).then_inc(V.sem, V.step((tag, "ones")))

            def begin(dve):
                vec_begin()
                vec_ones(dve)

            return pe, act, vec, begin, OH, OL, G4


        def rotary():
            C, W, H = C_ROT, W_ROT, H_ROT
            space, alloc = stage_memory()
            ln = ln_space(alloc)
            xb, xc, sq, dev = ln
            c = alloc("c", [P, C.n])
            WH, WL, p1, d1 = weights("w_rotary", W, alloc)
            HS, _, p2, d2 = weights("h_rotary", H, alloc, lo=False)
            sync, pool = stage_loads("rotary", c, p1 + p2, d1 + d2)
            npieces = len(p1) + len(p2)
            XH, XL = alloc("xq_hi", [P, KD, L], F32R), alloc("xq_lo", [P, KD, L], F32R)
            VH, VL = alloc("xkv_hi", [P, KD, L], F32R), alloc("xkv_lo", [P, KD, L], F32R)
            CH, CL = alloc("heads_hi", [P, 4, L], F32R), alloc("heads_lo", [P, 4, L], F32R)
            cm, sm, t0, t1, z, sqh, norm = (alloc(n, [P, L])[:, :] for n in ("cos_m", "sin_m", "t0", "t1", "z", "sq_head", "norm"))
            SEL = {"q": [lambda t: HS[:, H.of("qh", t)], lambda t: HS[:, H.of("ql", t)]],
                   "k": [lambda t: HS[:, H.of("kh", t)], lambda t: HS[:, H.of("kl", t)]],
                   "ident": HS[:, H.whole("ident")]}
            tag = "heads"
            a_pe, a_act, a_vec, a_begin, OH, OL, G4 = small_heads(
                alloc, tag, SH, SD, 64, lambda h: h, SD ** -0.5,
                lambda t: ((CH[:, t // 4, :], CL[:, t // 4, :], P), t % 4),
                lambda t: ((CH[:, 2 + t // 4, :], CL[:, 2 + t // 4, :], P), t % 4), SH // 2, c, C, None, SEL)
            space.close()
            KB = (2, 3, 4, 5)

            def pe(pe, s):
                pe.wait_ge(G.sem, G.at(("cut", first[s] + npieces - 1)))
                PE.enter(s)
                with pe.Fori(0, NB) as b:
                    round_start(pe, s, b)
                    ln_pe(pe, ln, s, b)
                    pe.wait_ge(A.sem, A.at((s, "xn squared"), b))
                    for k in range(KD):
                        last = nc.tensor.matmul(bank[2], ones[:, :], sq[:, k, :], start=k == 0, stop=k == KD - 1)
                    last.then_inc(PE.sem, PE.step((s, "norm2")))
                    ln_pe(pe, ln, s, b, " 2")
                    pe.wait_ge(V.sem, V.at((s, "xkv lo"), b))
                    for i in range(4):
                        name, hi, lo = ("wq", XH, XL) if i < 2 else ("wk", VH, VL)
                        for k in range(KD):
                            o = W.of(name, k, (i % 2) * P, (i % 2 + 1) * P)
                            last = mm3(bank[KB[i]], WH[:, o], WL[:, o], hi[:, k, :], lo[:, k, :], k == 0, k == KD - 1)
                        last.then_inc(PE.sem, PE.step((s, "qk", i)))
                    for i in range(4):
                        pe.wait_ge(V.sem, V.at((s, "turned", i), b))
                        nc.tensor.matmul(bank[6], c[:, C.whole("cen")], t0, start=True, stop=False)
                        nc.tensor.matmul(bank[6], c[:, C.whole("cenp")], t1, start=False, stop=True).then_inc(PE.sem, PE.step((s, "rotated", i)))
                        pe.wait_ge(A.sem, A.at((s, "head squared", i), b))
                        nc.tensor.matmul(bank[7], c[:, C.whole("blk")], sqh, start=True, stop=True).then_inc(PE.sem, PE.step((s, "head var", i)))

                    def value_product(psum, q):
                        if q == 0:
                            pe.wait_ge(V.sem, V.at((s, "heads lo"), b))
                        for k in range(KD):
                            o = W.of("wv", k)
                            xh, xl = VH[:, k, q * P:(q + 1) * P], VL[:, k, q * P:(q + 1) * P]
                            nc.tensor.matmul(psum[:, 0:D], xh, WH[:, o], start=k == 0, stop=False)
                            nc.tensor.matmul(psum[:, 0:D], xl, WH[:, o], start=False, stop=False)
                            nc.tensor.matmul(psum[:, 0:D], xh, WL[:, o], start=False, stop=False)
                        nc.tensor.matmul(psum[:, 0:D], ones[0:1, :], c[0:1, C.whole("bv")], start=False,
                                         stop=True).then_inc(PE.sem, PE.step((s, tag, ("v", q))))
                    a_pe(pe, s, b, value_product)
                    pe.wait_ge(A.sem, A.at((s, tag, "exp", G4 * QT * 2 - 1), b))
                    for g in range(G4):
                        pe.wait_ge(V.sem, V.at((s, tag, "o", g), b))
                        for m in range(KD):
                            o = W.of("wo", g, m * P, (m + 1) * P)
                            last = mm3(ps[0][:, m, :], WH[:, o], WL[:, o], OH[:, g, :], OL[:, g, :], g == 0, g == G4 - 1)
                    last.then_inc(PE.sem, PE.step((s, "out")))
                PE.leave(NB)

            def act(act, s):
                A.enter(s)
                with act.Fori(0, NB) as b:
                    round_start(act, s, b)
                    ln_act(act, ln, s, b)
                    act.wait_ge(V.sem, V.at((s, "xn"), b))
                    nc.scalar.activation(sq, xb, ACT.Square).then_inc(A.sem, A.step((s, "xn squared")))
                    act.wait_ge(PE.sem, PE.at((s, "norm2"), b))
                    nc.scalar.activation(norm, bank[2], ACT.Sqrt).then_inc(A.sem, A.step((s, "norm")))
                    ln_act(act, ln, s, b, " 2")
                    for i in range(4):
                        act.wait_ge(PE.sem, PE.at((s, "rotated", i), b))
                        nc.scalar.activation(sqh, bank[6], ACT.Square).then_inc(A.sem, A.step((s, "head squared", i)))
                        act.wait_ge(PE.sem, PE.at((s, "head var", i), b))
                        if i:
                            act.wait_ge(V.sem, V.at((s, "head done", i - 1), b))
                        nc.scalar.activation(z, bank[7], ACT.Sqrt, bias=eps_ln[:, :]).then_inc(A.sem, A.step((s, "head dev", i)))
                    a_act(act, s, b)
                A.leave(NB)

            def vec(dve, s):
                a_begin(dve)
                V.enter(s)
                with dve.Fori(0, NB) as b:
                    def after_last():
                        dve.wait_ge(V.sem, V.last(b))

                    round_start(dve, s, b)
                    ln_vec(dve, ln, s, b)
                    V.mark((s, "x in 2"))
                    dve.wait_ge(A.sem, A.at((s, "xn squared"), b))
                    ln_vec(dve, ln, s, b, " 2", load=False)
                    for g_, b_, hi, lo, what in (("gq", "bql", XH, XL, "xq lo"), ("gkv", "bkvl", VH, VL, "xkv lo")):
                        for k in range(KD):
                            after_last()
                            nc.vector.tensor_scalar(xc[:, k, :], xb[:, k, :], c[:, C.of(g_, 0, k, k + 1)], c[:, C.of(b_, 0, k, k + 1)],
                                                    ALU.mult, ALU.add).then_inc(V.sem, V.step())
                        after_last()
                        nc.vector.tensor_copy(hi[:, :, :], xc).then_inc(V.sem, V.step())
                        after_last()
                        nc.vector.tensor_tensor(lo[:, :, :], xc, hi[:, :, :].bitcast(F32), ALU.subtract).then_inc(V.sem, V.step((s, what)))
                    dve.wait_ge(A.sem, A.at((s, "norm"), b))
                    for m_, t_ in ((cm, "cos"), (sm, "sin")):
                        nc.vector.scalar_tensor_tensor(m_, norm, SD ** -0.25, c[:, C.whole(t_)], ALU.mult,
                                                       ALU.mult).then_inc(V.sem, V.step())
                    for i in range(4):
                        bias = c[:, C.of("bqk", 0, i, i + 1)]
                        dve.wait_ge(PE.sem, PE.at((s, "qk", i), b))
                        if i:
                            dve.wait_ge(PE.sem, PE.at((s, "rotated", i - 1), b))
                        after_last()
                        nc.vector.scalar_tensor_tensor(t0, bank[KB[i]], bias, cm, ALU.add, ALU.mult).then_inc(V.sem, V.step())
                        nc.vector.scalar_tensor_tensor(t1, bank[KB[i]], bias, sm, ALU.add, ALU.mult).then_inc(V.sem, V.step((s, "turned", i)))
                        dve.wait_ge(A.sem, A.at((s, "head dev", i), b))
                        nc.vector.reciprocal(z, z).then_inc(V.sem, V.step())
                        after_last()
                        nc.vector.tensor_tensor(z, z, bank[6], ALU.mult).then_inc(V.sem, V.step())
                        after_last()
                        nc.vector.tensor_scalar(norm, z, c[:, C.whole("gh")], c[:, C.whole("bh")], ALU.mult,
                                                ALU.add).then_inc(V.sem, V.step((s, "head done", i)))
                        after_last()
                        nc.vector.tensor_copy(CH[:, i, :], norm).then_inc(V.sem, V.step())
                        after_last()
                        nc.vector.tensor_tensor(CL[:, i, :], norm, CH[:, i, :].bitcast(F32), ALU.subtract).then_inc(V.sem, V.step((s, "heads lo")))
                    a_vec(dve, s, b)
                    dve.wait_ge(PE.sem, PE.at((s, "out"), b))
                    for m in range(KD):
                        after_last()
                        nc.vector.scalar_tensor_tensor(x[:, m, bass.ts(b, L)], ps[0][:, m, :], c[:, C.of("bo", 0, m, m + 1)],
                                                       x[:, m, bass.ts(b, L)], ALU.add, ALU.add).then_inc(V.sem, V.step())
                V.leave(NB)

            return {"sync": sync, "pool": pool, "pe": pe, "act": act, "vec": vec, "pieces": npieces}


        def gate_pe(pe, s, b, c, C, xb, own):
            pe.wait_ge(V.sem, V.at((s, "xn"), b))
            for bk, g in ((6, own), (7, 1 - own)):
                for k in range(KD):
                    last = nc.tensor.matmul(bank[bk], c[:, C.of("gatew", k, g * P, (g + 1) * P)], xb[:, k, :],
                                            start=k == 0, stop=k == KD - 1)
            last.then_inc(PE.sem, PE.step((s, "gate logits")))

        def gate_act(act, s, b, gt_):
            act.wait_ge(V.sem, V.at((s, "gate difference"), b))
            nc.scalar.activation(gt_, gt_, ACT.Exp).then_inc(A.sem, A.step((s, "gate exp")))

        def gate_vec(dve, s, b, c, C, gt_, own):
            dve.wait_ge(PE.sem, PE.at((s, "gate logits"), b))
            dve.wait_ge(V.sem, V.last(b))
            nc.vector.tensor_scalar(gt_, bank[6], c[:, C.of("gateb", 0, own, own + 1)], None, ALU.add).then_inc(V.sem, V.step())
            dve.wait_ge(V.sem, V.last(b))
            nc.vector.scalar_tensor_tensor(gt_, bank[7], c[:, C.of("gateb", 0, 1 - own, 2 - own)], gt_, ALU.add,
                                           ALU.subtract).then_inc(V.sem, V.step((s, "gate difference")))
            dve.wait_ge(A.sem, A.at((s, "gate exp"), b))
            nc.vector.tensor_scalar(gt_, gt_, 1.0, None, ALU.add).then_inc(V.sem, V.step())
            dve.wait_ge(V.sem, V.last(b))
            nc.vector.reciprocal(gt_, gt_).then_inc(V.sem, V.step((s, "gate")))

        def pattern():
            C, W, H = C_PAT, W_PAT, H_PAT
            space, alloc = stage_memory()
            ln = ln_space(alloc)
            xb, xc, sq, dev = ln
            c = alloc("c", [P, C.n])
            WH, WL, p1, d1 = weights("w_pattern", W, alloc)
            HS, _, p2, d2 = weights("h_pattern", H, alloc, lo=False)
            sync_in, pool = stage_loads("pattern", c, p1 + p2, d1 + d2)
            npieces = len(p1) + len(p2)
            XH, XL = alloc("xn_hi", [P, KD, L], F32R), alloc("xn_lo", [P, KD, L], F32R)
            CH, CL = alloc("heads_hi", [P, 4, L], F32R), alloc("heads_lo", [P, 4, L], F32R)
            gt_ = alloc("gate", [P, L])[:, :]
            SEL = {"q": [lambda t: HS[:, H.of("qh", t)], lambda t: HS[:, H.of("ql", t)]],
                   "k": [lambda t: HS[:, H.of("kh", t)], lambda t: HS[:, H.of("kl", t)]],
                   "ident": HS[:, H.whole("ident")]}
            tag = "heads"
            a_pe, a_act, a_vec, a_begin, OH, OL, G4 = small_heads(
                alloc, tag, SH, SD, 64, lambda h: h, SD ** -0.5,
                lambda t: ((CH[:, t // 4, :], CL[:, t // 4, :], P), t % 4),
                lambda t: ((CH[:, 2 + t // 4, :], CL[:, 2 + t // 4, :], P), t % 4), SH // 2, c, C, None, SEL)
            space.close()
            KB = (2, 3, 4, 5)

            def sync(sp, s):
                sync_in(sp, s)
                for b in range(NB):
                    sp.wait_ge(V.sem, V.at((s, "gated"), b))
                    sp.dma_start(gated_pattern[:, :, b * L:(b + 1) * L], xc).then_inc(kept, 16)
                    sp.wait_ge(kept, b * 16 + (16 + START))

            def pe(pe, s):
                pe.wait_ge(G.sem, G.at(("cut", first[s] + npieces - 1)))
                PE.enter(s)
                with pe.Fori(0, NB) as b:
                    round_start(pe, s, b)
                    ln_pe(pe, ln, s, b)
                    gate_pe(pe, s, b, c, C, xb, 1)
                    pe.wait_ge(V.sem, V.at((s, "xn lo"), b))
                    for i in range(4):
                        name = "wq" if i < 2 else "wk"
                        for k in range(KD):
                            o = W.of(name, k, (i % 2) * P, (i % 2 + 1) * P)
                            last = mm3(bank[KB[i]], WH[:, o], WL[:, o], XH[:, k, :], XL[:, k, :], k == 0, k == KD - 1)
                        last.then_inc(PE.sem, PE.step((s, "qk", i)))

                    def value_product(psum, q):
                        if q == 0:
                            pe.wait_ge(V.sem, V.at((s, "heads lo"), b))
                        for k in range(KD):
                            o = W.of("wv", k)
                            xh, xl = XH[:, k, q * P:(q + 1) * P], XL[:, k, q * P:(q + 1) * P]
                            nc.tensor.matmul(psum[:, 0:D], xh, WH[:, o], start=k == 0, stop=False)
                            nc.tensor.matmul(psum[:, 0:D], xl, WH[:, o], start=False, stop=False)
                            last = nc.tensor.matmul(psum[:, 0:D], xh, WL[:, o], start=False, stop=k == KD - 1)
                        last.then_inc(PE.sem, PE.step((s, tag, ("v", q))))
                    a_pe(pe, s, b, value_product)
                    pe.wait_ge(A.sem, A.at((s, tag, "exp", G4 * QT * 2 - 1), b))
                    for g in range(G4):
                        pe.wait_ge(V.sem, V.at((s, tag, "o", g), b))
                        for m in range(KD):
                            o = W.of("wo", g, m * P, (m + 1) * P)
                            last = mm3(ps[0][:, m, :], WH[:, o], WL[:, o], OH[:, g, :], OL[:, g, :], g == 0, g == G4 - 1)
                    last.then_inc(PE.sem, PE.step((s, "out")))
                PE.leave(NB)

            def act(act, s):
                A.enter(s)
                with act.Fori(0, NB) as b:
                    round_start(act, s, b)
                    ln_act(act, ln, s, b)
                    gate_act(act, s, b, gt_)
                    a_act(act, s, b)
                A.leave(NB)

            def vec(dve, s):
                a_begin(dve)
                V.enter(s)
                with dve.Fori(0, NB) as b:
                    def after_last():
                        dve.wait_ge(V.sem, V.last(b))

                    round_start(dve, s, b)
                    dve.wait_ge(kept, b * 16 + START)
                    ln_vec(dve, ln, s, b)
                    gate_vec(dve, s, b, c, C, gt_, 1)
                    nc.vector.tensor_copy(XH[:, :, :], xb).then_inc(V.sem, V.step())
                    after_last()
                    nc.vector.tensor_tensor(XL[:, :, :], xb, XH[:, :, :].bitcast(F32), ALU.subtract).then_inc(V.sem, V.step((s, "xn lo")))
                    for i in range(4):
                        dve.wait_ge(PE.sem, PE.at((s, "qk", i), b))
                        nc.vector.tensor_copy(CH[:, i, :], bank[KB[i]]).then_inc(V.sem, V.step())
                        after_last()
                        nc.vector.tensor_tensor(CL[:, i, :], bank[KB[i]], CH[:, i, :].bitcast(F32),
                                                ALU.subtract).then_inc(V.sem, V.step((s, "heads lo")))
                    a_vec(dve, s, b)
                    dve.wait_ge(PE.sem, PE.at((s, "out"), b))
                    for m in range(KD):
                        after_last()
                        nc.vector.tensor_tensor(xc[:, m, :], ps[0][:, m, :], gt_, ALU.mult).then_inc(V.sem, V.step((s, "gated")))
                V.leave(NB)

            return {"sync": sync, "pool": pool, "pe": pe, "act": act, "vec": vec, "pieces": npieces}


        def latent():
            C, W = C_LAT, W_LAT
            space, alloc = stage_memory()
            ln = ln_space(alloc)
            xb, xc, sq, dev = ln
            c = alloc("c", [P, C.n])
            WH, WL, p1, d1 = weights("w_latent", W, alloc)
            IDR = alloc("ident_r", [P, P], F32R)
            ONR = alloc("ones_r", [1, P], F32R)
            QNH, QNL = alloc("wqn_hi", [P, 2, HP, P], F32R), alloc("wqn_lo", [P, 2, HP, P], F32R)
            OVH, OVL = alloc("wov_hi", [P, HP, D], F32R), alloc("wov_lo", [P, HP, D], F32R)
            npieces = len(p1)
            before = ExitStack()
            comp = before.enter_context(nc.sbuf_tensor("composed_inputs", [P, M_LAT.n], F32))
            before.close()
            XH, XL = alloc("xn_hi", [P, KD, L], F32R), alloc("xn_lo", [P, KD, L], F32R)
            MH_, ML_ = alloc("qmid_hi", [P, 2, L], F32R), alloc("qmid_lo", [P, 2, L], F32R)
            KH, KL = alloc("k_hi", [P, 2, 2, L], F32R), alloc("k_lo", [P, 2, 2, L], F32R)
            QH, QL = alloc("q_hi", [P, 2, 2, L], F32R), alloc("q_lo", [P, 2, 2, L], F32R)
            MB = alloc("max_cols", [P, 2, QT, P], F32R)
            MR_ = alloc("max_rows", [1, 4, L], F32R)
            VT = alloc("v_tok", [P, QT, 2, P])
            PB = alloc("probs", [P, 2, 2, L])
            CX, DN = xc[:, 0, :], xc[:, 1, :]
            OH, OL = alloc("o_hi", [P, 2, L], F32R), alloc("o_lo", [P, 2, L], F32R)
            pe_raw = alloc("rope_raw", [P, L])[:, :]
            gt_ = alloc("gate", [P, L])[:, :]
            space.close()
            t0, t1 = sq[:, 0, :], sq[:, 1, :]
            main = xb
            lat = dev
            NPB = 2
            tag = "latent"

            def pair_aux(p):
                ev = [("kp", p), ("qn", p), ("kr", p), ("qp", p), ("qr", p)]
                for h in (2 * p, 2 * p + 1):
                    ev += [("mx", h, q) for q in range(QT)]
                ev += [("bias", 2 * p), ("bias", 2 * p + 1)]
                return ev

            units = [(p, kt) for p in range(HP) for kt in range(QT)]
            events, aux = pair_aux(0), []
            for n in range(len(units) + 1):
                if n < len(units):
                    p, kt = units[n]
                    if kt == 0:
                        aux += pair_aux(p + 1) if p + 1 < HP else []
                        share = -(-len(aux) // QT) if aux else 0
                    events.append(("s", p, kt))
                    for _ in range(min(share, len(aux))):
                        events.append(aux.pop(0))
                    if kt == QT - 1:
                        events += aux
                        aux = []
                if n:
                    p, kt = units[n - 1]
                    events.append(("pv", p, kt))
                    if kt == QT - 1:
                        events += [("sums", p), ("norm", p)]
                    if kt == 1 and p and p % 2 == 0:
                        events += [("out", p // 2 - 1, m) for m in range(KD)]
            events += [("out", HP // 2 - 1, m) for m in range(KD)]
            reader = {"kp": A, "kr": V, "qn": V, "qp": A, "qr": V, "mx": V, "bias": A, "out": V}
            aux_no, order = {}, []
            for ev in events:
                if ev[0] in reader:
                    aux_no[ev] = len(order)
                    order.append(ev)

            def slot(ev):
                return 4 + aux_no[ev] % 2

            def sync(sp, s):
                stage_start(sp, s, params=False)
                sp.dma_start(c[:, :], io["c_latent"]).then_inc(c_in, 16)
                sp.dma_start(comp[:, :], io["m_latent"]).then_inc(comp_in, 16)
                send_pieces(sp, p1, first[s])
                for b in range(NB):
                    sp.wait_ge(V.sem, V.at((s, tag, "o", HP - 1), b))
                    sp.dma_start(xc, gated_pattern[:, :, b * L:(b + 1) * L]).then_inc(fetched, 16)

            def pool(pool, s):
                stage_start(pool, s)
                cut_pieces(pool, d1, first[s])

            def pe(pe, s):
                pe.wait_ge(G.sem, G.at(("cut", first[s] + npieces - 1)))
                pe.wait_ge(comp_in, 16)
                n = 0
                for t in range(2):
                    for half in range(2):
                        bk = n % 8
                        for i in range(8):
                            h = half * 8 + i
                            last = nc.tensor.matmul(bank[bk][:, i * 64:(i + 1) * 64],
                                                    comp[:, M_LAT.of("wqn", 0, h * 2 * P + t * P, h * 2 * P + (t + 1) * P)],
                                                    comp[:, M_LAT.of("wkn", 0, h * 64, (h + 1) * 64)], start=True, stop=True)
                        last.then_inc(PE.sem, PE.step((s, "composed", n)))
                        n += 1
                for p in range(HP):
                    if n >= 8:
                        pe.wait_ge(V.sem, V.at((s, "composed cut", n - 8)))
                    for i in (0, 1):
                        h = 2 * p + i
                        last = nc.tensor.matmul(bank[n % 8][64 * i:64 * i + 64, 0:D],
                                                comp[:, M_LAT.of("wvn", 0, h * 64, (h + 1) * 64)],
                                                comp[:, M_LAT.of("wot", 0, h * D, (h + 1) * D)], start=True, stop=True)
                    last.then_inc(PE.sem, PE.step((s, "composed", n)))
                    n += 1
                PE.enter(s)
                with pe.Fori(0, NB) as b:
                    round_start(pe, s, b)
                    ln_pe(pe, ln, s, b)
                    gate_pe(pe, s, b, c, C, xb, 0)
                    pe.wait_ge(V.sem, V.at((s, "xn lo"), b))
                    for m in range(3):
                        for k in range(KD):
                            o = W.of("qa", k, m * P, (m + 1) * P) if m < 2 else W.of("kva", k)
                            last = mm3(bank[2 + m], WH[:, o], WL[:, o], XH[:, k, :], XL[:, k, :], k == 0, k == KD - 1)
                        last.then_inc(PE.sem, PE.step((s, "middle", m)))
                    pe.wait_ge(A.sem, A.at((s, "middle squared"), b))
                    for k in range(2):
                        last = nc.tensor.matmul(bank[0], ones[:, :], sq[:, k, :], start=k == 0, stop=k == 1)
                    last.then_inc(PE.sem, PE.step((s, "q power")))
                    pe.wait_ge(A.sem, A.at((s, "latent squared"), b))
                    nc.tensor.matmul(bank[1], ones[:, :], pe_raw, start=True, stop=True).then_inc(PE.sem, PE.step((s, "kv power")))
                    pe.wait_ge(V.sem, V.at((s, "latent"), b))
                    for q in range(QT):
                        last = nc.tensor.transpose(bank[5][:, q * P:(q + 1) * P], lat[:, q * P:(q + 1) * P],
                                                   c[:, C.whole("ident")])
                    last.then_inc(PE.sem, PE.step((s, "latent turned")))
                    pe.wait_ge(V.sem, V.at((s, "ready"), b))
                    pe.wait_ge(A.sem, A.at((s, "latent tokens"), b))
                    for ev in events:
                        kind = ev[0]
                        by_act, by_vec = [], []
                        if kind in reader and aux_no[ev] >= 2:
                            old = order[aux_no[ev] - 2]
                            (by_act if reader[old[0]] is A else by_vec).append((s, tag, old))
                        if kind == "kr":
                            by_act.append((s, tag, ("kp", ev[1])))
                        if kind == "qr":
                            by_act.append((s, tag, ("qp", ev[1])))
                        if kind == "mx" and ev[2] == 0 and ev[1] % 2 == 0:
                            by_vec.append((s, tag, ("qr", ev[1] // 2)))
                        if kind == "bias":
                            by_vec.append((s, tag, ("mx", ev[1], QT - 1)))
                        if kind == "s":
                            n = ev[1] * QT + ev[2]
                            if ev[2] == 0:
                                by_act.append((s, tag, ("bias", 2 * ev[1] + 1)))
                            if n >= 2:
                                by_act.append((s, tag, "exp", n - 2))
                        if kind == "pv":
                            by_act.append((s, tag, "exp", ev[1] * QT + ev[2]))
                            if ev[2] == 0 and ev[1]:
                                by_act.append((s, tag, ("sums", ev[1] - 1)))
                        if kind == "out":
                            by_vec.append((s, tag, "o", 2 * ev[1] + 1))
                        if by_act:
                            pe.wait_ge(A.sem, A.at(later(A, *by_act), b))
                        if by_vec:
                            pe.wait_ge(V.sem, V.at(later(V, *by_vec), b))
                        last = None
                        if kind in ("kp", "qp", "qn"):
                            p = ev[1]
                            for k in range(2):
                                if kind == "qn":
                                    wh, wl = QNH[:, k, p, :], QNL[:, k, p, :]
                                else:
                                    o = W.of("kpe" if kind == "kp" else "qpe", k, p * P, (p + 1) * P)
                                    wh, wl = WH[:, o], WL[:, o]
                                hi, lo = (XH, XL) if kind == "kp" else (MH_, ML_)
                                last = mm3(bank[slot(ev)], wh, wl, hi[:, k, :], lo[:, k, :], k == 0, k == 1)
                        elif kind in ("kr", "qr"):
                            last = nc.tensor.matmul(bank[slot(ev)], c[:, C.whole("rot")], pe_raw, start=True, stop=True)
                        elif kind == "mx":
                            h, q = ev[1:]
                            last = nc.tensor.matmul(bank[slot(ev)], QH[:, (h // 2) % 2, h % 2, q * P:(q + 1) * P],
                                                    KH[:, (h // 2) % 2, h % 2, :], start=True, stop=True)
                        elif kind == "bias":
                            for q in range(QT):
                                last = nc.tensor.matmul(bank[slot(ev)][:, q * P:(q + 1) * P], MB[:, ev[1] % 2, q, :],
                                                        IDR[:, :], start=True, stop=True)
                        elif kind == "s":
                            p, kt = ev[1:]
                            n = p * QT + kt
                            for i in (0, 1):
                                o = slice(kt * P, (kt + 1) * P)
                                mm3(ps[n % 2][:, i, :], KH[:, p % 2, i, o], KL[:, p % 2, i, o], QH[:, p % 2, i, :],
                                    QL[:, p % 2, i, :], True, False)
                                last = nc.tensor.matmul(ps[n % 2][:, i, :], ONR[0:1, :], MR_[0:1, (p % 2) * 2 + i, :],
                                                        start=False, stop=True)
                        elif kind == "pv":
                            p, kt = ev[1:]
                            for i in (0, 1):
                                last = nc.tensor.matmul(bank[6 + i], VT[:, kt, i, :], PB[:, (p * QT + kt) % NPB, i, :],
                                                        start=kt == 0, stop=kt == QT - 1)
                        elif kind == "out":
                            pp, m = ev[1:]
                            for i in (0, 1):
                                p = 2 * pp + i
                                last = mm3(bank[slot(ev)], OVH[:, p, m * P:(m + 1) * P], OVL[:, p, m * P:(m + 1) * P],
                                           OH[:, i, :], OL[:, i, :], i == 0, i == 1)
                        if last is not None:
                            last.then_inc(PE.sem, PE.step((s, tag, ev)))
                PE.leave(NB)

            def act(act, s):
                A.enter(s)
                with act.Fori(0, NB) as b:
                    round_start(act, s, b)
                    ln_act(act, ln, s, b)
                    gate_act(act, s, b, gt_)
                    act.wait_ge(PE.sem, PE.at((s, "middle", 2), b))
                    nc.scalar.activation(sq, ps[1][:, :, :], ACT.Square).then_inc(A.sem, A.step((s, "middle squared")))
                    nc.scalar.activation(pe_raw, bank[4], ACT.Square).then_inc(A.sem, A.step((s, "latent squared")))
                    act.wait_ge(PE.sem, PE.at((s, "q power"), b))
                    nc.scalar.activation(CX, bank[0], ACT.Sqrt, bias=eps_rms[:, :], scale=1.0 / AQR).then_inc(A.sem, A.step())
                    act.wait_ge(PE.sem, PE.at((s, "kv power"), b))
                    nc.scalar.activation(DN, bank[1], ACT.Sqrt, bias=eps_rms[:, :],
                                         scale=1.0 / (2 * AKR)).then_inc(A.sem, A.step((s, "deviations")))
                    act.wait_ge(PE.sem, PE.at((s, "latent turned"), b))
                    for i in (0, 1):
                        nc.scalar.activation(VT[:, :, i, 64 * i:64 * i + 64], bank[5][:, :].rearrange("p (q d) -> p q d", d=P)[:, :, 64 * i:64 * i + 64],
                                             ACT.Copy).then_inc(A.sem, A.step((s, "latent tokens")))
                    act.wait_ge(V.sem, V.at((s, "ready"), b))
                    for ev in events:
                        kind = ev[0]
                        if kind in ("kp", "qp"):
                            if kind == "kp" and ev[1]:
                                act.wait_ge(V.sem, V.at((s, tag, ("qr", ev[1] - 1)), b))
                            if kind == "qp":
                                act.wait_ge(V.sem, V.at((s, tag, ("kr", ev[1])), b))
                            act.wait_ge(PE.sem, PE.at((s, tag, ev), b))
                            nc.scalar.activation(pe_raw, bank[slot(ev)], ACT.Copy).then_inc(A.sem, A.step((s, tag, ev)))
                        elif kind == "bias":
                            h = ev[1]
                            act.wait_ge(PE.sem, PE.at((s, tag, ev), b))
                            nc.scalar.activation(MR_[0:1, h % 4, :], bank[slot(ev)][0:1, :], ACT.Copy).then_inc(A.sem, A.step((s, tag, ev)))
                        elif kind == "s":
                            n = ev[1] * QT + ev[2]
                            act.wait_ge(PE.sem, PE.at((s, tag, ev), b))
                            nc.scalar.activation(PB[:, n % NPB, :, :], ps[n % 2][:, :, :], ACT.Exp,
                                                 scale=AQ ** -0.5).then_inc(A.sem, A.step((s, tag, "exp", n)))
                        elif kind == "sums":
                            p = ev[1]
                            act.wait_ge(PE.sem, PE.at((s, tag, ("pv", p, QT - 1)), b))
                            if p:
                                act.wait_ge(V.sem, V.at((s, tag, "o", p - 1), b))
                            for i in (0, 1):
                                r, r2 = slice(64 * i, 64 * i + 64), slice(64 - 64 * i, 128 - 64 * i)
                                nc.scalar.activation(CX[r, :], bank[6 + i][r, :], ACT.Copy).then_inc(A.sem, A.step())
                                nc.scalar.activation(DN[r, :], bank[6 + i][r2, :], ACT.Copy).then_inc(A.sem, A.step((s, tag, ev)))
                A.leave(NB)

            def vec(dve, s):
                nc.vector.memset(MB[:, :, :, :].bitcast(F32), 0.0).then_inc(V.sem, V.step())
                nc.vector.memset(VT[:, :, :, :], 1.0).then_inc(V.sem, V.step())
                nc.vector.tensor_copy(IDR[:, :], c[:, C.whole("ident")]).then_inc(V.sem, V.step())
                nc.vector.tensor_copy(ONR[:, :], ones[0:1, :]).then_inc(V.sem, V.step())
                n = 0
                for t in range(2):
                    for half in range(2):
                        dve.wait_ge(PE.sem, PE.at((s, "composed", n)))
                        src = bank[n % 8][:, :].rearrange("p (q i) -> p q i", i=P)
                        o = slice(half * 4, half * 4 + 4)
                        nc.vector.tensor_copy(QNH[:, t, o, :], src).then_inc(V.sem, V.step())
                        dve.wait_ge(V.sem, V.last())
                        nc.vector.tensor_tensor(QNL[:, t, o, :], src, QNH[:, t, o, :].bitcast(F32),
                                                ALU.subtract).then_inc(V.sem, V.step((s, "composed cut", n)))
                        n += 1
                for p in range(HP):
                    dve.wait_ge(PE.sem, PE.at((s, "composed", n)))
                    nc.vector.tensor_copy(OVH[:, p, :], bank[n % 8][:, 0:D]).then_inc(V.sem, V.step())
                    dve.wait_ge(V.sem, V.last())
                    nc.vector.tensor_tensor(OVL[:, p, :], bank[n % 8][:, 0:D], OVH[:, p, :].bitcast(F32),
                                            ALU.subtract).then_inc(V.sem, V.step((s, "composed cut", n)))
                    n += 1
                V.enter(s)
                with dve.Fori(0, NB) as b:
                    def after_last():
                        dve.wait_ge(V.sem, V.last(b))

                    round_start(dve, s, b)
                    ln_vec(dve, ln, s, b)
                    gate_vec(dve, s, b, c, C, gt_, 0)
                    nc.vector.tensor_copy(XH[:, :, :], xb).then_inc(V.sem, V.step())
                    after_last()
                    nc.vector.tensor_tensor(XL[:, :, :], xb, XH[:, :, :].bitcast(F32), ALU.subtract).then_inc(V.sem, V.step((s, "xn lo")))
                    dve.wait_ge(A.sem, A.at((s, "deviations"), b))
                    nc.vector.reciprocal(CX, CX).then_inc(V.sem, V.step())
                    nc.vector.reciprocal(DN, DN).then_inc(V.sem, V.step())
                    after_last()
                    for k in range(2):
                        nc.vector.scalar_tensor_tensor(sq[:, k, :], bank[2 + k], c[:, C.of("qln", 0, k, k + 1)], CX,
                                                       ALU.mult, ALU.mult).then_inc(V.sem, V.step())
                    nc.vector.scalar_tensor_tensor(lat, bank[4], c[:, C.whole("kvln")], DN, ALU.mult,
                                                   ALU.mult).then_inc(V.sem, V.step((s, "latent")))
                    after_last()
                    nc.vector.tensor_copy(MH_[:, :, :], sq).then_inc(V.sem, V.step())
                    after_last()
                    nc.vector.tensor_tensor(ML_[:, :, :], sq, MH_[:, :, :].bitcast(F32), ALU.subtract).then_inc(V.sem, V.step())
                    for sl in (0, 1):
                        for i in (0, 1):
                            r = slice(64 * i, 64 * i + 64)
                            nc.vector.tensor_copy(KH[r, sl, i, :], lat[r, :]).then_inc(V.sem, V.step())
                            after_last()
                            nc.vector.tensor_tensor(KL[r, sl, i, :], lat[r, :], KH[r, sl, i, :].bitcast(F32),
                                                    ALU.subtract).then_inc(V.sem, V.step((s, "ready")))
                    for ev in events:
                        kind = ev[0]
                        if kind in ("kr", "qr"):
                            p = ev[1]
                            dve.wait_ge(PE.sem, PE.at((s, tag, ev), b))
                            nc.vector.tensor_tensor(t0, c[:, C.whole("sin")], bank[slot(ev)], ALU.mult).then_inc(V.sem, V.step())
                            nc.vector.tensor_tensor(t1, pe_raw, c[:, C.whole("cos")], ALU.mult).then_inc(V.sem, V.step())
                            after_last()
                            nc.vector.tensor_tensor(t0, t0, t1, ALU.add).then_inc(V.sem, V.step())
                            after_last()
                            hi, lo = (KH, KL) if kind == "kr" else (QH, QL)
                            for i in (0, 1):
                                r = slice(64 - 64 * i, 128 - 64 * i)
                                nc.vector.tensor_copy(hi[r, p % 2, i, :], t0[r, :]).then_inc(V.sem, V.step())
                            after_last()
                            for i in (0, 1):
                                r = slice(64 - 64 * i, 128 - 64 * i)
                                nc.vector.tensor_tensor(lo[r, p % 2, i, :], t0[r, :], hi[r, p % 2, i, :].bitcast(F32),
                                                        ALU.subtract).then_inc(V.sem, V.step((s, tag, ev)))
                            after_last()
                        elif kind == "qn":
                            p = ev[1]
                            dve.wait_ge(PE.sem, PE.at((s, tag, ev), b))
                            for i in (0, 1):
                                r = slice(64 * i, 64 * i + 64)
                                nc.vector.tensor_copy(QH[r, p % 2, i, :], bank[slot(ev)][r, :]).then_inc(V.sem, V.step())
                            after_last()
                            for i in (0, 1):
                                r = slice(64 * i, 64 * i + 64)
                                nc.vector.tensor_tensor(QL[r, p % 2, i, :], bank[slot(ev)][r, :], QH[r, p % 2, i, :].bitcast(F32),
                                                        ALU.subtract).then_inc(V.sem, V.step((s, tag, ev)))
                        elif kind == "mx":
                            h, q = ev[1:]
                            dve.wait_ge(PE.sem, PE.at((s, tag, ev), b))
                            nc.vector.tensor_reduce(MB[:, h % 2, q, 0:1], bank[slot(ev)], op=ALU.max, axis=AX.X,
                                                    negate=True).then_inc(V.sem, V.step((s, tag, ev)))
                        elif kind == "norm":
                            p = ev[1]
                            dve.wait_ge(A.sem, A.at((s, tag, ("sums", p)), b))
                            nc.vector.reciprocal(DN, DN).then_inc(V.sem, V.step())
                            after_last()
                            nc.vector.tensor_tensor(CX, CX, DN, ALU.mult).then_inc(V.sem, V.step())
                            after_last()
                            if p >= 2:
                                dve.wait_ge(PE.sem, PE.at((s, tag, ("out", p // 2 - 1, KD - 1)), b))
                            nc.vector.tensor_copy(OH[:, p % 2, :], CX).then_inc(V.sem, V.step())
                            after_last()
                            nc.vector.tensor_tensor(OL[:, p % 2, :], CX, OH[:, p % 2, :].bitcast(F32),
                                                    ALU.subtract).then_inc(V.sem, V.step((s, tag, "o", p)))
                        elif kind == "out":
                            pp, m = ev[1:]
                            dve.wait_ge(PE.sem, PE.at((s, tag, ev), b))
                            if pp:
                                nc.vector.tensor_tensor(main[:, m, :], main[:, m, :], bank[slot(ev)], ALU.add).then_inc(V.sem, V.step((s, tag, ev)))
                            else:
                                nc.vector.tensor_copy(main[:, m, :], bank[slot(ev)]).then_inc(V.sem, V.step((s, tag, ev)))
                    for m in range(KD):
                        after_last()
                        nc.vector.tensor_tensor(main[:, m, :], main[:, m, :], gt_, ALU.mult).then_inc(V.sem, V.step())
                    dve.wait_ge(fetched, b * 16 + (16 + START))
                    after_last()
                    nc.vector.tensor_tensor(main, main, xc, ALU.add).then_inc(V.sem, V.step())
                    after_last()
                    nc.vector.tensor_tensor(x[:, :, bass.ts(b, L)], x[:, :, bass.ts(b, L)], main, ALU.add).then_inc(V.sem, V.step())
                V.leave(NB)

            return {"sync": sync, "pool": pool, "pe": pe, "act": act, "vec": vec, "pieces": npieces}


        def grouped():
            C, W, H = C_GRP, W_GRP, H_GRP
            KV = BH * BD
            space, alloc = stage_memory()
            ln = ln_space(alloc)
            xb, xc, sq, dev = ln
            c = alloc("c", [P, C.n])
            WH, WL, p1, d1 = weights("w_grouped", W, alloc)
            HS, _, p2, d2 = weights("h_grouped", H, alloc, lo=False)
            sync, pool = stage_loads("grouped", c, p1 + p2, d1 + d2)
            npieces = len(p1) + len(p2)
            XH, XL = alloc("xn_hi", [P, KD, L], F32R), alloc("xn_lo", [P, KD, L], F32R)
            CH, CL = alloc("heads_hi", [P, 3, L], F32R), alloc("heads_lo", [P, 3, L], F32R)
            mix = alloc("mix", [P, 3])
            el = alloc("elu", [P, KD, L])[:, :, :]
            am = alloc("memory_out", [P, KD, L])[:, :, :]
            t0 = alloc("t0", [P, L])[:, :]
            SEL = {"q": [lambda t: HS[:, H.of("qh", t)], lambda t: HS[:, H.of("ql", t)]],
                   "k": [lambda t: HS[:, H.of("kh", t)], lambda t: HS[:, H.of("kl", t)]],
                   "ident": HS[:, H.whole("ident")]}
            tag = "heads"
            a_pe, a_act, a_vec, a_begin, OH, OL, G4 = small_heads(
                alloc, tag, BQ * BH, BD, 32, lambda h: h % BH, BD ** -0.5,
                lambda t: ((CH[:, t // 4, :], CL[:, t // 4, :], P), t % 4),
                lambda t: ((CH[:, 2, :], CL[:, 2, :], P), t % 2), BH // 4, c, C, None, SEL)
            space.close()
            QB = (2, 3, 4)

            def pe(pe, s):
                pe.wait_ge(G.sem, G.at(("cut", first[s] + npieces - 1)))
                PE.enter(s)
                with pe.Fori(0, NB) as b:
                    round_start(pe, s, b)
                    ln_pe(pe, ln, s, b)
                    pe.wait_ge(V.sem, V.at((s, "xn lo"), b))
                    for i in range(3):
                        name = "wq" if i < 2 else "wk"
                        for k in range(KD):
                            o = W.of(name, k, (i % 2) * P, (i % 2 + 1) * P)
                            last = mm3(bank[QB[i]], WH[:, o], WL[:, o], XH[:, k, :], XL[:, k, :], k == 0, k == KD - 1)
                        last.then_inc(PE.sem, PE.step((s, "qk", i)))
                    for m in range(KD):
                        pe.wait_ge(V.sem, V.at((s, "elu", m), b))
                        if m:
                            pe.wait_ge(V.sem, V.at((s, "answer", m - 1), b))
                        nc.tensor.matmul(bank[0], c[:, C.whole("mem")], el[:, m, :], start=True, stop=True)
                        nc.tensor.matmul(bank[1], c[:, C.whole("memn")], el[:, m, :], start=True,
                                         stop=True).then_inc(PE.sem, PE.step((s, "memory", m)))

                    def value_product(psum, q):
                        if q == 0:
                            pe.wait_ge(V.sem, V.at((s, "answer", KD - 1), b))
                        for k in range(KD):
                            o = W.of("wv", k)
                            xh, xl = XH[:, k, q * P:(q + 1) * P], XL[:, k, q * P:(q + 1) * P]
                            nc.tensor.matmul(psum[:, 0:KV], xh, WH[:, o], start=k == 0, stop=False)
                            nc.tensor.matmul(psum[:, 0:KV], xl, WH[:, o], start=False, stop=False)
                            last = nc.tensor.matmul(psum[:, 0:KV], xh, WL[:, o], start=False, stop=k == KD - 1)
                        last.then_inc(PE.sem, PE.step((s, tag, ("v", q))))
                    a_pe(pe, s, b, value_product)
                    pe.wait_ge(A.sem, A.at((s, tag, "exp", G4 * QT * 2 - 1), b))
                    for g in range(G4):
                        pe.wait_ge(V.sem, V.at((s, tag, "o", g), b))
                        m, i = divmod(g, G4 // KD)
                        perm = HS[:, H.of("perm", i)]
                        nc.tensor.matmul(ps[0][:, m, :], perm, OH[:, g, :], start=i == 0, stop=False)
                        last = nc.tensor.matmul(ps[0][:, m, :], perm, OL[:, g, :], start=False, stop=i == G4 // KD - 1)
                    last.then_inc(PE.sem, PE.step((s, "out")))
                PE.leave(NB)

            def act(act, s):
                nc.scalar.activation(mix[:, 2:3], c[:, C.whole("memw")], ACT.Exp, scale=-1.0).then_inc(A.sem, A.step((s, "exp w")))
                A.enter(s)
                with act.Fori(0, NB) as b:
                    round_start(act, s, b)
                    ln_act(act, ln, s, b)
                    for m in range(KD):
                        act.wait_ge(V.sem, V.at((s, "negative", m), b))
                        nc.scalar.activation(el[:, m, :], am[:, m, :], ACT.Tanh, scale=0.5).then_inc(A.sem, A.step((s, "tanh", m)))
                    a_act(act, s, b)
                A.leave(NB)

            def vec(dve, s):
                a_begin(dve)
                dve.wait_ge(A.sem, A.at((s, "exp w")))
                nc.vector.tensor_scalar(mix[:, 2:3], mix[:, 2:3], 1.0, None, ALU.add).then_inc(V.sem, V.step())
                dve.wait_ge(V.sem, V.last())
                nc.vector.reciprocal(mix[:, 0:1], mix[:, 2:3]).then_inc(V.sem, V.step())
                dve.wait_ge(V.sem, V.last())
                nc.vector.tensor_scalar(mix[:, 1:2], mix[:, 0:1], -1.0, 1.0, ALU.mult, ALU.add).then_inc(V.sem, V.step())
                V.enter(s)
                with dve.Fori(0, NB) as b:
                    def after_last():
                        dve.wait_ge(V.sem, V.last(b))

                    round_start(dve, s, b)
                    ln_vec(dve, ln, s, b)
                    after_last()
                    nc.vector.tensor_copy(XH[:, :, :], xb).then_inc(V.sem, V.step())
                    after_last()
                    nc.vector.tensor_tensor(XL[:, :, :], xb, XH[:, :, :].bitcast(F32), ALU.subtract).then_inc(V.sem, V.step((s, "xn lo")))
                    for i in range(3):
                        dve.wait_ge(PE.sem, PE.at((s, "qk", i), b))
                        nc.vector.tensor_copy(CH[:, i, :], bank[QB[i]]).then_inc(V.sem, V.step())
                        if i < 2:
                            nc.vector.tensor_scalar(am[:, i, :], bank[QB[i]], 0.0, None, ALU.min).then_inc(V.sem, V.step((s, "negative", i)))
                        after_last()
                        nc.vector.tensor_tensor(CL[:, i, :], bank[QB[i]], CH[:, i, :].bitcast(F32),
                                                ALU.subtract).then_inc(V.sem, V.step((s, "heads lo")))
                    for m in range(KD):
                        dve.wait_ge(A.sem, A.at((s, "tanh", m), b))
                        nc.vector.tensor_scalar(t0, el[:, m, :], -1.0, 1.0, ALU.mult, ALU.add).then_inc(V.sem, V.step())
                        after_last()
                        nc.vector.reciprocal(t0, t0).then_inc(V.sem, V.step())
                        after_last()
                        nc.vector.scalar_tensor_tensor(t0, el[:, m, :], 2.0, t0, ALU.mult, ALU.mult).then_inc(V.sem, V.step())
                        after_last()
                        nc.vector.scalar_tensor_tensor(el[:, m, :], bank[QB[m]], 0.0, t0, ALU.max,
                                                       ALU.add).then_inc(V.sem, V.step((s, "elu", m)))
                        after_last()
                    for m in range(KD):
                        dve.wait_ge(PE.sem, PE.at((s, "memory", m), b))
                        nc.vector.reciprocal(t0, bank[1]).then_inc(V.sem, V.step())
                        after_last()
                        nc.vector.scalar_tensor_tensor(am[:, m, :], bank[0], mix[:, 0:1], t0, ALU.mult,
                                                       ALU.mult).then_inc(V.sem, V.step((s, "answer", m)))
                        after_last()
                    a_vec(dve, s, b)
                    dve.wait_ge(PE.sem, PE.at((s, "out"), b))
                    for m in range(KD):
                        after_last()
                        nc.vector.scalar_tensor_tensor(am[:, m, :], ps[0][:, m, :], mix[:, 1:2], am[:, m, :], ALU.mult,
                                                       ALU.add).then_inc(V.sem, V.step())
                    after_last()
                    nc.vector.tensor_tensor(x[:, :, bass.ts(b, L)], x[:, :, bass.ts(b, L)], am, ALU.add).then_inc(V.sem, V.step())
                V.leave(NB)

            return {"sync": sync, "pool": pool, "pe": pe, "act": act, "vec": vec, "pieces": npieces}


        makers = {
            "ffn0": lambda: ffn(0),
            "ffn1": lambda: ffn(1),
            "mamba": mamba,
            "rotary": rotary,
            "pattern": pattern,
            "latent": latent,
            "grouped": grouped,
        }
        stages = [makers[name]() for name in plan]
        first = [sum(st["pieces"] for st in stages[:s]) for s in range(len(stages))]

        block = ctx.enter_context(nc.Block())

        @block.sync
        def _(sp):
            sp.sem_inc(kept, START)
            sp.sem_inc(fetched, START)
            sp.dma_start(x[:, :, :], io["x"]).then_inc(x_in, 16)
            for s, stage in enumerate(stages):
                stage["sync"](sp, s)
            sp.wait_ge(V.sem, V.at(("end", len(stages) - 1)))
            sp.dma_start(out, x[:, :, :]).then_inc(stored, 16)
            sp.wait_ge(stored, 16)

        @block.gpsimd
        def _(pool):
            nc.gpsimd.memset(c256[:, :], 1.0 / D).then_inc(G.sem, START - 3)
            nc.gpsimd.memset(ones[:, :], 1.0).then_inc(G.sem, 1)
            nc.gpsimd.memset(eps_ln[:, :], LN_EPS).then_inc(G.sem, 1)
            nc.gpsimd.memset(eps_rms[:, :], RMS_EPS).then_inc(G.sem, 1)
            for s, stage in enumerate(stages):
                stage["pool"](pool, s)
                G.mark(("end", s))

        @block.tensor
        def _(pe):
            pe.sem_inc(PE.sem, START)
            pe.wait_ge(G.sem, START)
            for s, stage in enumerate(stages):
                stage_start(pe, s)
                stage["pe"](pe, s)
                PE.mark(("end", s))

        @block.scalar
        def _(act):
            act.sem_inc(A.sem, START)
            act.wait_ge(G.sem, START)
            for s, stage in enumerate(stages):
                stage_start(act, s)
                stage["act"](act, s)
                A.mark(("end", s))

        @block.vector
        def _(dve):
            dve.sem_inc(V.sem, START)
            dve.wait_ge(G.sem, START)
            dve.wait_ge(x_in, 16)
            for s, stage in enumerate(stages):
                stage_start(dve, s)
                stage["vec"](dve, s)
                V.mark(("end", s))


PLAN = ("mamba", "ffn0", "rotary", "ffn0", "pattern", "latent", "ffn1", "grouped", "ffn1")


def host_ffn(j, arrays, put):
    E, I, S, nt = E_[j], I_[j], S_[j], NT[j]
    if j == 0:
        cat = lambda e, s_: np.concatenate([np.asarray(e).transpose(1, 0, 2).reshape(D, -1), np.asarray(s_)], 1)
        gate, up = cat(arrays["L0_ffn_w_gate"], arrays["L0_ffn_sw_gate"]), cat(arrays["L0_ffn_w_up"], arrays["L0_ffn_sw_up"])
        down = np.concatenate([np.asarray(arrays["L0_ffn_w_down"]).reshape(-1, D), arrays["L0_ffn_sw_down"]], 0)
        router = arrays["L0_ffn_router_w"]
    else:
        gu, sgu = np.asarray(arrays["L1_ffn_expert_gate_up"]), np.asarray(arrays["L1_ffn_shared_gate_up"])
        gate = np.concatenate([gu[:, :I].reshape(-1, D), sgu[:S]], 0).T
        up = np.concatenate([gu[:, I:].reshape(-1, D), sgu[S:]], 0).T
        down = np.concatenate([np.asarray(arrays["L1_ffn_expert_down"]).transpose(0, 2, 1).reshape(-1, D),
                               np.asarray(arrays["L1_ffn_shared_down"]).T], 0)
        router = np.concatenate([np.asarray(arrays["L1_ffn_gate_w"]).T, np.asarray(arrays["L1_ffn_shared_gate_vec"]).T], 1)
    n = gate.shape[1]
    NE = E + j
    w = np.zeros((nt, P, TW + P), np.float32)
    for t in range(nt):
        c0, c1 = t * P, min((t + 1) * P, n)
        for k in range(KD):
            w[t, :, (2 * k) * P:(2 * k) * P + c1 - c0] = gate[k * P:(k + 1) * P, c0:c1]
            w[t, :, (2 * k + 1) * P:(2 * k + 1) * P + c1 - c0] = up[k * P:(k + 1) * P, c0:c1]
        w[t, :c1 - c0, KD * 2 * P:TW] = down[c0:c1]
        for i in range(c0, c1):
            e = min(i // I, E)
            if e < NE:
                w[t, [e, NE + e], TW + i - c0] = 1.0
    put(f"w_ffn{j}", w)
    C = C_FFN[j]
    c = np.zeros((P, C.n), np.float32)
    C.put(c, "router", router)
    C.put(c, "iota", np.tile(np.arange(E, dtype=np.float32), (P, QT)))
    C.put(c, "ident", np.eye(P, dtype=np.float32))
    put(f"c_ffn{j}", c)


def columns(v):
    return np.asarray(v).reshape(-1, P).T


def host_mamba(arrays, put):
    a = {n[len("L0_attn_a_"):]: np.asarray(v) for n, v in arrays.items() if n.startswith("L0_attn_a_")}
    w = np.zeros((P, W_MAMBA.n), np.float32)
    W_MAMBA.put(w, "wx", a["W_in_x"].T)
    W_MAMBA.put(w, "wz", a["W_in_z"].T)
    W_MAMBA.put(w, "wp", a["W_param"].T)
    W_MAMBA.put(w, "wo", a["W_out"].T)
    put("w_mamba", w)
    h = np.zeros((P, H_MAMBA.n), np.float32)
    H_MAMBA.put(h, "expand", np.repeat(np.eye(MH, dtype=np.float32), MN, axis=1))
    put("h_mamba", h)
    C = C_MAMBA
    c = np.zeros((P, C.n), np.float32)
    C.put(c, "conv_w", a["conv_w"].reshape(MT, P, MK).transpose(1, 0, 2).reshape(P, MT * MK))
    C.put(c, "conv_b", columns(a["conv_b"]))
    C.put(c, "A_log", columns(a["A_log"].reshape(-1)))
    C.put(c, "Dp", columns(a["D"]))
    C.put(c, "b_dt", a["b_dt"].reshape(MH, 1))
    C.put(c, "wdt", a["W_dt"].T)
    put("c_mamba", c)


def stacking(H, packed, rows, width, patterns, prefix=""):
    places = {"qh": (0, 2), "ql": (1,), "kh": (0, 1), "kl": (2,)}
    for name, blocks in places.items():
        k = H.at[prefix + name][1]
        for t in range(k):
            sel = np.zeros((P, P), np.float32)
            for i, r0 in enumerate(patterns[t]):
                for blk in blocks:
                    for d in range(width):
                        sel[r0 + d, i * rows + blk * width + d] = 1.0
            packed[:, H.of(prefix + name, t)] = sel


def stacked_out(w, width):
    heads = w.shape[0] // width
    out = np.zeros((heads, 32, w.shape[1]), np.float32)
    out[:, :width] = np.asarray(w).reshape(heads, width, -1)
    return out.reshape(heads * 32, -1)


def head_constants(C, c, rows, width):
    one = np.zeros((P, 1), np.float32)
    one[3 * width::rows] = 1.0
    C.put(c, "one_row", one)
    den = np.zeros((P, P), np.float32)
    for j in range(4):
        den[32 * j + width, 32 * j:32 * j + 32] = 1.0
    C.put(c, "den", den)


def host_rotary(arrays, put):
    a = {n[len("L0_attn_b_"):]: np.asarray(v) for n, v in arrays.items() if n.startswith("L0_attn_b_")}
    w = np.zeros((P, W_ROT.n), np.float32)
    W_ROT.put(w, "wq", a["Wq"])
    W_ROT.put(w, "wk", a["Wkv"][:, :D])
    W_ROT.put(w, "wv", a["Wkv"][:, D:])
    W_ROT.put(w, "wo", stacked_out(a["Wo"], SD))
    put("w_rotary", w)
    h = np.zeros((P, H_ROT.n), np.float32)
    stacking(H_ROT, h, 64, SD, [(2 * t * SD, (2 * t + 1) * SD) for t in range(4)])
    H_ROT.put(h, "ident", np.eye(P, dtype=np.float32))
    put("h_rotary", h)
    C = C_ROT
    c = np.zeros((P, C.n), np.float32)
    for name, v in (("gq", "ln_q_g"), ("bql", "ln_q_b"), ("gkv", "ln_kv_g"), ("bkvl", "ln_kv_b"), ("bo", "bo")):
        C.put(c, name, columns(a[v]))
    C.put(c, "bqk", np.concatenate([columns(a["bq"]), columns(a["bkv"][:D])], 1))
    C.put(c, "gh", np.tile(a["ln_h_g"].reshape(SD, 1), (P // SD, 1)))
    C.put(c, "bh", np.tile(a["ln_h_b"].reshape(SD, 1), (P // SD, 1)))
    C.put(c, "bv", a["bkv"][D:].reshape(1, D))
    head_constants(C, c, 64, SD)
    f = np.float32(8000.0 / 200.0) ** np.linspace(0.0, 1.0, SD // 2, dtype=np.float32) * np.float32(200.0) / np.float32(1000.0)
    f = np.float32(200.0) * f / np.float32(1000.0)
    ang = (np.arange(L, dtype=np.float32)[None] * f.astype(np.float32)[:, None]).astype(np.float32)
    ang = np.tile(np.repeat(ang, 2, axis=0), (P // SD, 1))
    C.put(c, "cos", np.cos(ang).astype(np.float32))
    C.put(c, "sin", np.sin(ang).astype(np.float32))
    blk = np.kron(np.eye(P // SD), np.full((SD, SD), 1.0 / SD))
    cen = np.eye(P) - blk
    turn = np.kron(np.eye(P // 2), np.array([[0.0, -1.0], [1.0, 0.0]]))
    C.put(c, "blk", blk.T.astype(np.float32))
    C.put(c, "cen", cen.T.astype(np.float32))
    C.put(c, "cenp", (cen @ turn).T.astype(np.float32))
    put("c_rotary", c)


def rope_pairs(w, heads, width, first_row, rows):
    w = np.asarray(w)
    out = []
    for p in range(heads // 2):
        for h in (2 * p + 1, 2 * p):
            out.append(w[h * width + first_row:h * width + first_row + rows])
    return np.concatenate(out, 0).T


def host_pattern(arrays, put):
    a = {n[len("L1_attn_a_"):]: np.asarray(v) for n, v in arrays.items() if n.startswith("L1_attn_a_")}
    w = np.zeros((P, W_PAT.n), np.float32)
    W_PAT.put(w, "wq", a["sp_q_w"].T)
    W_PAT.put(w, "wk", a["sp_k_w"].T)
    W_PAT.put(w, "wv", a["sp_v_w"].T)
    W_PAT.put(w, "wo", stacked_out(a["sp_o_w"].T, SD))
    put("w_pattern", w)
    h = np.zeros((P, H_PAT.n), np.float32)
    stacking(H_PAT, h, 64, SD, [(2 * t * SD, (2 * t + 1) * SD) for t in range(4)])
    H_PAT.put(h, "ident", np.eye(P, dtype=np.float32))
    put("h_pattern", h)
    c = np.zeros((P, C_PAT.n), np.float32)
    gate_constants(C_PAT, c, a)
    head_constants(C_PAT, c, 64, SD)
    put("c_pattern", c)


def gate_constants(C, c, a):
    C.put(c, "gatew", np.repeat(a["gate_w"].T, P, axis=1))
    C.put(c, "gateb", np.repeat(a["gate_b"].reshape(1, 2), P, axis=0))


def host_latent(arrays, put):
    a = {n[len("L1_attn_a_"):]: np.asarray(v) for n, v in arrays.items() if n.startswith("L1_attn_a_")}
    w = np.zeros((P, W_LAT.n), np.float32)
    W_LAT.put(w, "qa", np.concatenate([a["q_a_w"].T, np.zeros((D, D - AQR), np.float32)], 1))
    W_LAT.put(w, "kva", np.concatenate([a["kv_a_w"][:AKR].T] * 2, 1))
    W_LAT.put(w, "kpe", rope_pairs(a["kv_a_w"][AKR:], AH, AROPE, 0, AROPE))
    W_LAT.put(w, "qpe", rope_pairs(a["q_b_w"], AH, AQ, ANOPE, AROPE))
    put("w_latent", w)
    m = np.zeros((P, M_LAT.n), np.float32)
    qn = np.zeros((P, AH, 2 * P), np.float32)
    qn[:, :, :AQR] = a["q_b_w"].reshape(AH, AQ, AQR)[:, :ANOPE].transpose(1, 0, 2)
    kv = a["kv_b_w"].reshape(AH, ANOPE + AV, AKR)
    M_LAT.put(m, "wqn", qn.reshape(P, -1))
    M_LAT.put(m, "wkn", kv[:, :ANOPE].transpose(1, 0, 2).reshape(P, -1))
    M_LAT.put(m, "wvn", kv[:, ANOPE:].transpose(1, 0, 2).reshape(P, -1))
    M_LAT.put(m, "wot", a["o_w"].T.reshape(AH, AV, D).transpose(1, 0, 2).reshape(P, -1))
    put("m_latent", m)
    C = C_LAT
    c = np.zeros((P, C.n), np.float32)
    gate_constants(C, c, a)
    qln = np.zeros((2 * P,), np.float32)
    qln[:AQR] = a["q_a_ln_w"]
    C.put(c, "qln", columns(qln))
    C.put(c, "kvln", np.concatenate([a["kv_a_ln_w"]] * 2).reshape(P, 1))
    C.put(c, "ident", np.eye(P, dtype=np.float32))
    inv = (1.0 / np.float32(10000.0) ** (np.arange(0, AROPE, 2, dtype=np.float32) / np.float32(AROPE))).astype(np.float32)
    ang = (np.arange(L, dtype=np.float32)[None] * inv[:, None]).astype(np.float32)
    C.put(c, "cos", np.tile(np.cos(ang).astype(np.float32), (4, 1)))
    sin = np.sin(ang).astype(np.float32)
    C.put(c, "sin", np.tile(np.concatenate([-sin, sin], 0), (2, 1)))
    swap = np.kron(np.eye(2), np.kron(np.array([[0.0, 1.0], [1.0, 0.0]]), np.eye(AROPE // 2)))
    C.put(c, "rot", swap.astype(np.float32))
    put("c_latent", c)


def host_grouped(arrays, put):
    a = {n[len("L1_attn_b_"):]: np.asarray(v) for n, v in arrays.items() if n.startswith("L1_attn_b_")}
    KV = BH * BD
    w = np.zeros((P, W_GRP.n), np.float32)
    W_GRP.put(w, "wq", a["Wq"].T)
    W_GRP.put(w, "wk", np.concatenate([a["Wk"].T, np.zeros((D, P - KV), np.float32)], 1))
    W_GRP.put(w, "wv", a["Wv"].T)
    put("w_grouped", w)
    h = np.zeros((P, H_GRP.n), np.float32)
    stacking(H_GRP, h, 32, BD, [[(t // 2) * KV + ((t % 2) * 4 + i) * BD for i in range(4)] for t in range(4)])
    H_GRP.put(h, "ident", np.eye(P, dtype=np.float32))
    for g in range(4):
        perm = np.zeros((P, P), np.float32)
        for i in range(4):
            for d in range(BD):
                perm[32 * i + d, (g // 2) * KV + ((g % 2) * 4 + i) * BD + d] = 1.0
        h[:, H_GRP.of("perm", g)] = perm
    put("h_grouped", h)
    C = C_GRP
    c = np.zeros((P, C.n), np.float32)
    mem, memn = np.zeros((P, P), np.float32), np.zeros((P, P), np.float32)
    for i in range(P // KV):
        mem[i * KV:(i + 1) * KV, i * KV:(i + 1) * KV] = a["memory"]
        memn[i * KV:(i + 1) * KV, i * KV:(i + 1) * KV] = np.repeat(a["memory_norm"], KV, axis=1)
    C.put(c, "mem", mem)
    C.put(c, "memn", memn)
    C.put(c, "memw", np.repeat(a["memory_weight"].reshape(1, 1), P, axis=0))
    head_constants(C, c, 32, BD)
    put("c_grouped", c)


HOST = {
    "ffn0": lambda a, p: host_ffn(0, a, p),
    "ffn1": lambda a, p: host_ffn(1, a, p),
    "mamba": host_mamba,
    "rotary": host_rotary,
    "pattern": host_pattern,
    "latent": host_latent,
    "grouped": host_grouped,
}


def kernel(**inputs):
    import concourse.bacc as bacc
    from concourse.bass_utils import run_bass_kernel_spmd

    arrays = {}
    xt = np.asarray(inputs["L0_attn_a_hidden_states"]).reshape(T, KD, P).transpose(2, 1, 0)
    arrays["x"] = np.ascontiguousarray(xt)

    def put(name, a):
        arrays[name] = np.ascontiguousarray(a)

    for name in dict.fromkeys(PLAN):
        HOST[name](inputs, put)

    def program(table):
        nc = bacc.Bacc("TRN2", target_bir_lowering=False, num_devices=1)
        io = {n: nc.dram_tensor(f"in_{n}", a.shape, F32, kind="ExternalInput").ap() for n, a in arrays.items()}
        out = nc.dram_tensor("out_0", (P, KD, T), F32, kind="ExternalOutput").ap()
        build(nc, io, out, PLAN, table)
        return nc

    table = {}
    program(table)
    nc = program(table)
    r = run_bass_kernel_spmd(nc, [{f"in_{n}": a for n, a in arrays.items()}], core_ids=[0])
    y = r.results[0]["out_0"]
    return y.transpose(2, 1, 0).reshape(NB, L, D)
```
